# Optimizing a Trainium2 kernel written in Bass

```python
import numpy as np
import jax
import jax.numpy as jnp

def _softmax(x, axis=-1):
    return jax.nn.softmax(x, axis=axis)

def _gelu(x):
    return jax.nn.gelu(x, approximate=True)

def _silu(x):
    return jax.nn.silu(x)

def _sigmoid(x):
    return jax.nn.sigmoid(x)

def _layernorm(x, axis=-1, eps=1e-05):
    m = jnp.mean(x, axis=axis, keepdims=True)
    v = jnp.var(x, axis=axis, keepdims=True)
    return (x - m) / jnp.sqrt(v + eps)

def _scatter_add(tgt, idx, src, axis=0):
    return tgt.at[idx].add(src)

def _segment_sum(src, seg, n):
    return jax.ops.segment_sum(src, seg, n)
kernel_name = 'mk_sandwich_d1_jaxref_r8_4c7486'

def setup_inputs(seed: int=0):
    np.random.seed(seed)
    _w = jnp.asarray

    def _L0_attn_setup():
        import jax, jax.numpy as jnp
        import numpy as np
        Bsz, L, D, N = (2, 256, 128, 16)
        LN_EPS = 1e-05
        key = jax.random.key(seed)
        ks = jax.random.split(key, 5)
        A_log = -jnp.broadcast_to(jnp.log(jnp.arange(1, N + 1, dtype=jnp.float32))[None, :], (D, N))
        return {'x': jax.random.normal(ks[0], (Bsz, L, D), jnp.float32), 'W_dt': jax.random.normal(ks[1], (D, D), jnp.float32) * 0.02, 'b_dt': jnp.zeros((D,), jnp.float32), 'W_B': jax.random.normal(ks[2], (N, D), jnp.float32) * 0.02, 'W_C': jax.random.normal(ks[3], (N, D), jnp.float32) * 0.02, 'D_param': jnp.ones((D,), jnp.float32), 'A_log': A_log, 'gamma': jnp.ones((D,), jnp.float32), 'beta': jnp.zeros((D,), jnp.float32)}
    _L0_attn_in = _L0_attn_setup()

    def _L0_ffn_setup():
        import jax, jax.numpy as jnp
        import numpy as np
        B, S, D, H, E = (2, 256, 128, 512, 8)
        TOP_K = 2
        key = jax.random.key(seed)
        ks = jax.random.split(key, 5)
        scale = 0.02
        return {'x': jax.random.normal(ks[0], (B, S, D), dtype=jnp.float32), 'gate_w': jax.random.normal(ks[1], (D, E), dtype=jnp.float32) * scale, 'gate_b': jnp.zeros((E,), dtype=jnp.float32), 'w1': jax.random.normal(ks[2], (E, D, H), dtype=jnp.float32) * scale, 'b1': jnp.zeros((E, H), dtype=jnp.float32), 'w2': jax.random.normal(ks[3], (E, H, D), dtype=jnp.float32) * scale, 'b2': jnp.zeros((E, D), dtype=jnp.float32)}
    _L0_ffn_in = _L0_ffn_setup()
    _d = {'L0_attn_x': _L0_attn_in['x'], 'L0_attn_W_dt': _L0_attn_in['W_dt'], 'L0_attn_b_dt': _L0_attn_in['b_dt'], 'L0_attn_W_B': _L0_attn_in['W_B'], 'L0_attn_W_C': _L0_attn_in['W_C'], 'L0_attn_D_param': _L0_attn_in['D_param'], 'L0_attn_A_log': _L0_attn_in['A_log'], 'L0_attn_gamma': _L0_attn_in['gamma'], 'L0_attn_beta': _L0_attn_in['beta'], 'L0_ffn_gate_w': _L0_ffn_in['gate_w'], 'L0_ffn_gate_b': _L0_ffn_in['gate_b'], 'L0_ffn_w1': _L0_ffn_in['w1'], 'L0_ffn_b1': _L0_ffn_in['b1'], 'L0_ffn_w2': _L0_ffn_in['w2'], 'L0_ffn_b2': _L0_ffn_in['b2']}
    _x0 = _d['L0_attn_x']
    _d['L0_attn_x'] = jax.random.normal(jax.random.fold_in(jax.random.key(seed), 1), (8, 512, 128), dtype=_x0.dtype)
    del _x0
    return _d

def reference(L0_attn_x, L0_attn_W_dt, L0_attn_b_dt, L0_attn_W_B, L0_attn_W_C, L0_attn_D_param, L0_attn_A_log, L0_attn_gamma, L0_attn_beta, L0_ffn_gate_w, L0_ffn_gate_b, L0_ffn_w1, L0_ffn_b1, L0_ffn_w2, L0_ffn_b2):

    def _L0_attn_ref(x, W_dt, b_dt, W_B, W_C, D_param, A_log, gamma, beta):
        import jax, jax.numpy as jnp
        import numpy as np
        Bsz, L, D, N = (2, 256, 128, 16)
        LN_EPS = 1e-05
        residual = x
        mu = jnp.mean(x, axis=-1, keepdims=True)
        var = jnp.var(x, axis=-1, keepdims=True)
        xn = (x - mu) * jax.lax.rsqrt(var + LN_EPS) * gamma + beta
        dt = jax.nn.softplus(xn @ W_dt.T + b_dt)
        A = -jnp.exp(A_log)
        B_in = xn @ W_B.T
        C_in = xn @ W_C.T
        A_bar = jnp.exp(dt[..., None] * A)
        Bx = dt[..., None] * B_in[:, :, None, :] * xn[..., None]

        def step(h, inputs):
            a_t, bx_t, c_t = inputs
            h = a_t * h + bx_t
            y_t = jnp.einsum('bn,bdn->bd', c_t, h)
            return (h, y_t)
        h0 = jnp.zeros((x.shape[0], D, N), x.dtype)
        _, ys = jax.lax.scan(step, h0, (jnp.transpose(A_bar, (1, 0, 2, 3)), jnp.transpose(Bx, (1, 0, 2, 3)), jnp.transpose(C_in, (1, 0, 2))))
        y = jnp.transpose(ys, (1, 0, 2)) + D_param * residual
        return y

    def _L0_ffn_ref(x, gate_w, gate_b, w1, b1, w2, b2):
        import jax, jax.numpy as jnp
        import numpy as np
        B, S, D, H, E = (2, 256, 128, 512, 8)
        TOP_K = 2
        gate_logits = jnp.einsum('bsd,de->bse', x, gate_w) + gate_b
        gate_weights = jax.nn.softmax(gate_logits, axis=-1)
        topk_values, topk_indices = jax.lax.top_k(gate_weights, TOP_K)
        hidden = jax.nn.relu(jnp.einsum('bsd,edh->bseh', x, w1) + b1)
        expert_out = jnp.einsum('bseh,ehd->bsed', hidden, w2) + b2
        sel = jnp.take_along_axis(expert_out, topk_indices[..., None], axis=2)
        return jnp.sum(topk_values[..., None] * sel, axis=2)
    x = L0_attn_x
    x = x + _layernorm(_L0_attn_ref(_layernorm(x, axis=-1), L0_attn_W_dt, L0_attn_b_dt, L0_attn_W_B, L0_attn_W_C, L0_attn_D_param, L0_attn_A_log, L0_attn_gamma, L0_attn_beta), axis=-1)
    x = x + _layernorm(_L0_ffn_ref(_layernorm(x, axis=-1), L0_ffn_gate_w, L0_ffn_gate_b, L0_ffn_w1, L0_ffn_b1, L0_ffn_w2, L0_ffn_b2), axis=-1)
    return x

_drawn_inputs = setup_inputs


def setup_inputs(seed=0):
    import zlib

    import numpy as np

    out = dict(_drawn_inputs(seed))
    spreads = {'L0_attn_b_dt': (0.0, 0.1),
     'L0_attn_D_param': (1.0, 0.2),
     'L0_attn_gamma': (1.0, 0.2),
     'L0_attn_beta': (0.0, 0.1),
     'L0_ffn_gate_b': (0.0, 0.1),
     'L0_ffn_b1': (0.0, 0.1),
     'L0_ffn_b2': (0.0, 0.1)}
    factors = {}
    for name, (base, spread) in spreads.items():
        noise = np.random.default_rng([zlib.crc32(name.encode()), seed]).standard_normal(out[name].shape)
        drawn = base * np.exp(spread * noise) if base else spread * noise
        out[name] = jnp.asarray(drawn.astype(out[name].dtype))
    for name, factor in factors.items():
        out[name] = (out[name] * factor).astype(out[name].dtype)
    return out
```

```python
from contextlib import ExitStack

import concourse.bass as bass
from concourse import mybir

F32 = mybir.dt.float32
F32R = mybir.dt.float32r
BF16 = mybir.dt.bfloat16
I32 = mybir.dt.int32
U32 = mybir.dt.uint32
ALU = mybir.AluOpType
ACT = mybir.ActivationFunctionType
AX = mybir.AxisListType

P = 128
EPS = 1e-5
SEQS, T, D, N = 8, 512, 128, 16
E, HID, TOPK = 8, 512, 2
K = T // P
J = P // N
UNITS = D // J
TILES = K * TOPK + E - 1
SLOTS = TILES * P
HC = HID // P
NX = 5
NO = 3
assert TILES % NX == 0 and TILES % NO == 0
ROUTE_LINKS = 28
NU = 4
NBIAS = E * HID + E * D + D
BC = NBIAS // P
B2_AT, BDT_AT = E * HID, E * HID + E * D
LAST_LAG = 4


def order():
    prep = {0: "load", 3: "stats", 5: "norm", 6: "turn", 7: "states", 8: "readout", 9: "delta", 10: "split"}
    post = {1: "reload", 4: "y_sum", 6: "y_norm", 8: "x1_norm", 10: "gate_turn", 12: "gate_logits", 13: "route"}
    scatter = {13: (0, 2), 14: (2, 4), 15: (4, 6), 16: (6, 8)}
    gather = {6: (0, 2), 7: (2, 4), 8: (4, 6), 9: (6, 8)}
    tile = ("tile_load", -2), ("tile_turn", 3), ("tile_up", 4), ("tile_fold", 5), ("tile_down", 6)
    steps = []
    for half in (0, 1):
        for u in range(UNITS):
            for kind, lag in (("rep", 0), ("decay", 0), ("drive", 0), ("scan", 1), ("weigh", 1)):
                steps.append((kind, half - 1 - (u < lag), (u - lag) % UNITS))
            if u in post:
                steps.append((post[u], half - 2))
            steps.append(("reduce", half - 1 - (u < 4), (u - 4) % UNITS))
            if u in prep:
                steps.append((prep[u], half))
            if half == 1 and u < E:
                steps.append(("weights", 1, u))
            for v in (u, u + UNITS):
                late = v // UNITS
                if v in scatter:
                    steps.append(("scatter", half - 2 - late, *scatter[v]))
            for late in (-1, 0, 1):
                for kind, lag in tile[::-1]:
                    j = u + UNITS * late - lag
                    if 0 <= j < TILES:
                        steps.append((kind, half - 3 - late, j))
            if u in gather:
                steps.append(("gather", half - 4, *gather[u]))
            if u == 12:
                steps.append(("combine", half - 4))
    return steps


def program(nc, x, w_dt_t, w_bc_t, biases, d_param, a_log, gamma, beta, gate_w, gate_b, w1, w2, out):
    slots_in = [nc.dram_tensor(f"slots_in{i}", [SLOTS, D], F32, kind="Internal").ap() for i in range(2)]
    slots_out = [nc.dram_tensor(f"slots_out{i}", [SLOTS, D], F32, kind="Internal").ap() for i in range(2)]
    bias_rows = nc.dram_tensor("bias_rows", [3, NBIAS], BF16, kind="Internal").ap()
    x_in = x.rearrange("b (k p) d -> b p k d", p=P)
    x_out = out.rearrange("b (k p) d -> b p k d", p=P)

    with ExitStack() as ctx:
        def sb(name, shape, dt=F32):
            return ctx.enter_context(nc.sbuf_tensor(name, shape, dt))

        def bank(name):
            return ctx.enter_context(nc.psum_tensor(name, [P, 512], F32))

        ident = sb("ident", [P, P])
        ones = sb("ones", [P, P])
        before = sb("before", [P, P])
        spread_f = sb("spread_f", [P, J, N, J])
        spread = sb("spread", [P, J, P], F32R)
        fold_f = sb("fold_f", [P, N, J])
        fold = sb("fold", [P, J])
        ones_b = sb("ones_b", [3, 512], BF16)
        iota_i = sb("iota_i", [P, K * E], I32)
        iota_k = sb("iota_k", [P, E * K], I32)
        iota_e = sb("iota_e", [P, K, E])
        restart = sb("restart", [P, E, K])
        iota_ji = sb("iota_ji", [1, TILES * E], I32)
        iota_j = sb("iota_j", [1, TILES, E])
        eps = sb("eps", [P, 2])
        w_dt = sb("w_dt", [D, D])
        w_bc = sb("w_bc", [D, 2 * N])
        w_rep = sb("w_rep", [D, 2, N, J])
        decay = sb("decay", [P, UNITS])
        gam = sb("gam", [D, 1])
        bet = sb("bet", [D, 1])
        skip = sb("skip", [P, D])
        gate = sb("gate", [D, E])
        gate_bias = sb("gate_bias", [P, E])
        bias_f = sb("bias_f", [P, BC])
        bias_r = sb("bias_r", [P, BC])
        bias_s = sb("bias_s", [P, BC])
        bias_parts = sb("bias_parts", [P, 3, BC], BF16)
        bias = sb("bias", [3, NBIAS], BF16)
        w1_f = sb("w1_f", [P, 2, HID])
        w2_f = sb("w2_f", [P, E * HC * D])
        w_hi = sb("w_hi", [P, E * HID], F32R)
        w_lo = sb("w_lo", [P, E * HID], F32R)
        zeros = sb("zeros", [P, D])

        xs = sb("xs", [P, 2, K, D])
        xr = sb("xr", [P, K, D])
        st = sb("st", [P, K, 6])
        mv = sb("mv", [P, 2, K, 2])
        lv = sb("lv", [P, 2, K])
        rs = sb("rs", [P, 2, 2, K])
        u_t = sb("u_t", [P, 2, K, D])
        xn = sb("xn", [P, 2, K, D])
        xa = sb("xa", [D, 2, T])
        sp_l = sb("sp_l", [D, T])
        dt = sb("dt", [D, T])
        gx = sb("gx", [D, T])
        dt_hi = sb("dt_hi", [D, T], F32R)
        dt_lo = sb("dt_lo", [D, T], F32R)
        gx_hi = sb("gx_hi", [D, T], F32R)
        gx_lo = sb("gx_lo", [D, T], F32R)
        dt_s = sb("dt_s", [P, 2, 2, T], F32R)
        gx_s = sb("gx_s", [P, 2, 2, T], F32R)
        b_rep = sb("b_rep", [P, 2, T])
        c_rep = sb("c_rep", [P, 2, T])
        ab = sb("ab", [P, 2, T])
        bx = sb("bx", [P, 2, T])
        hs = sb("hs", [P, NU, T])
        ch = sb("ch", [P, NU, T])
        y = sb("y", [P, K, D])
        st_y = sb("st_y", [P, K, 6])
        mv_y = sb("mv_y", [P, K, 2])
        lv_y = sb("lv_y", [P, K])
        rs_y = sb("rs_y", [P, K])
        st_1 = sb("st_1", [P, K, 6])
        mv_1 = sb("mv_1", [P, K, 2])
        lv_1 = sb("lv_1", [P, K])
        rs_1 = sb("rs_1", [P, K])
        x1 = sb("x1", [P, SEQS * K, D])
        x2 = sb("x2", [P, 2, K, D])
        x2_t = sb("x2_t", [D, T])
        logit = sb("logit", [P, K, E])
        r_max = sb("r_max", [P, K])
        r_sub = sb("r_sub", [P, K, E])
        r_exp = sb("r_exp", [P, K, E])
        r_sum = sb("r_sum", [P, K])
        prob = sb("prob", [P, K, E])
        eq = sb("eq", [P, K, E])
        cand = sb("cand", [P, K, E])
        pick = sb("pick", [P, K])
        hot = sb("hot", [P, TOPK, K, E])
        prob_2 = sb("prob_2", [P, K, E])
        mask = sb("mask", [P, K, E])
        tot = sb("tot", [P, E, K])
        run = sb("run", [P, E, K])
        cnt_i = sb("cnt_i", [P, E], I32)
        til_i = sb("til_i", [P, E], I32)
        til = sb("til", [P, E])
        end = sb("end", [P, E])
        beg = sb("beg", [P, E])
        pos_a = sb("pos_a", [P, E, K])
        pos_b = sb("pos_b", [P, E, K])
        pos_e = sb("pos_e", [P, K, E])
        pos_h = sb("pos_h", [P, TOPK * K, E])
        pos_f = sb("pos_f", [P, TOPK * K])
        pos = sb("pos", [P, 2, TOPK * K], U32)
        weight = sb("weight", [P, 2, TOPK, K])
        past = sb("past", [1, TILES, E])
        exp_f = sb("exp_f", [1, TILES])
        expert = sb("expert", [1, 2, TILES], I32)
        xt = sb("xt", [P, NX, D])
        xt_hi = sb("xt_hi", [D, 2, P], F32R)
        xt_lo = sb("xt_lo", [D, 2, P], F32R)
        hid = sb("hid", [P, 2, HID])
        hid_t = sb("hid_t", [P, 2, HID])
        ot = sb("ot", [P, NO, D])
        yg = sb("yg", [P, TOPK, K, D])
        mix = sb("mix", [P, K, D])
        st_m = sb("st_m", [P, K, 6])
        mv_m = sb("mv_m", [P, K, 2])
        lv_m = sb("lv_m", [P, K])
        rs_m = sb("rs_m", [P, K])

        dt_ps = bank("dt_ps")
        gx_ps = bank("gx_ps")
        y_ps = bank("y_ps")
        misc = bank("misc")
        turn = bank("turn")
        out_ps = bank("out_ps")
        hid_ps = bank("hid_ps")
        fold_ps = bank("fold_ps")

        names = """consts results_free pool_set mix_half route_done prefix_used dve_set small bias_ld bias_split bias_out bias_in w_ld w_split_hi w_split_lo w_rep_set
            decay_exp decay_set zero_set zeroed iota_set
            stats moments logs scales normed turned xa_ready b_ps b_ready c_ps c_ready z_ps sp_abs sp_exp sp_log
            dt_ready gx_ready dt_hi_ready gx_hi_ready dt_lo_ready gx_lo_ready
            dt_rep gx_rep decayed driven scanned weighed reduced
            skip_ready y_ready y_stats y_mom y_log y_scale y_normed x1_ready x1_stats x1_mom x1_log x1_scale x2_ready
            x_reloaded x2_turned x2_copied logits_ps logits_ready route_chain route_max route_exp mask_ready prefix_ready routed
            tile_turned tile_hi tile_lo tile_hid tile_relu tile_folded fold_copied tile_out tile_copied
            mix_ready mix_stats mix_mom mix_log mix_scale out_ready written""".split()
        s = {n: ctx.enter_context(nc.semaphore(n)) for n in names}
        x_loaded = [ctx.enter_context(nc.semaphore(f"x_loaded{i}")) for i in range(2)]
        tile_loaded = [ctx.enter_context(nc.semaphore(f"tile_loaded{i}")) for i in range(NX)]
        stacked = [ctx.enter_context(nc.semaphore(f"stacked{i}")) for i in range(2)]
        scattered = [ctx.enter_context(nc.semaphore(f"scattered{i}")) for i in range(2)]
        gathered = [ctx.enter_context(nc.semaphore(f"gathered{i}")) for i in range(2)]
        w1_loaded = [ctx.enter_context(nc.semaphore(f"w1_loaded{i}")) for i in range(2)]
        stored = [ctx.enter_context(nc.semaphore(f"stored{i}")) for i in range(NO)]
        steps = order()

        def after(eng, sem, n):
            if not (isinstance(n, int) and n <= 0):
                eng.wait_ge(sem, n)

        def alone(eng, *waits):
            for _, n in waits:
                if not isinstance(n, int):
                    eng.compute_val(n)
            eng.wait_ge(s["consts"], 1)
            for sem, n in waits:
                after(eng, sem, n)

        def chain(eng, sem, per, index):
            n = [0]

            def link(ins):
                n[0] += 1
                ins.then_inc(sem, 1)
                eng.wait_ge(sem, per * index + n[0])
            return link

        def turns(per, b, i):
            return per // 2 * (b - i)

        def tile_seen(b, j, n):
            return TILES * b + (j - n + 1 if j >= n else 0)

        def walk(eng, parts):
            def iteration(it, first, last):
                for kind, c, *args in steps:
                    if kind in parts and 2 * first + c >= 0 and 2 * last + c < SEQS and (
                            kind != "weights" or last == 0):
                        parts[kind](2 * it + c, c % 2, *args)

            ahead = LAST_LAG // 2
            for it in range(ahead):
                iteration(it, it, it)
            with eng.Fori(ahead, SEQS // 2) as it:
                iteration(it, ahead, SEQS // 2 - 1)
            for it in range(SEQS // 2, SEQS // 2 + ahead):
                iteration(it, it, it)

        block = ctx.enter_context(nc.Block())

        @block.sync
        def _(sp):
            def load(b, i):
                alone(sp, (s["skip_ready"], 2 * b - 3))
                sp.dma_start(xs[:, i], x_in[b]).then_inc(x_loaded[i], 16)

            def reload(b, i):
                alone(sp, (s["x1_ready"], b))
                sp.dma_start(xr[:], x_in[b]).then_inc(s["x_reloaded"], 16)

            def weights(b, i, c):
                if c + 2 < E:
                    sp.wait_ge(s["w_split_lo"], c + 1)
                    sp.dma_start(w1_f[:, c % 2], w1[c + 2]).then_inc(w1_loaded[c % 2], 16)

            def split(b, i):
                if not isinstance(b, int):
                    sp.compute_val(b + 1)
                alone(sp, (s["dt_rep"], UNITS * (b - 1)), (s["gx_rep"], UNITS * (b - 1)))
                for hi, lo, hi_sem, lo_sem, dst in ((dt_hi, dt_lo, s["dt_hi_ready"], s["dt_lo_ready"], dt_s),
                                                    (gx_hi, gx_lo, s["gx_hi_ready"], s["gx_lo_ready"], gx_s)):
                    alone(sp, (hi_sem, b + 1))
                    for h in range(2):
                        sp.dma_start(dst[0:64, i, h].bitcast(F32), hi[64 * h:64 * h + 64, :].bitcast(F32)).then_inc(stacked[i], 16)
                    alone(sp, (lo_sem, b + 1))
                    for h in range(2):
                        sp.dma_start(dst[64:128, i, h].bitcast(F32), lo[64 * h:64 * h + 64, :].bitcast(F32)).then_inc(stacked[i], 16)

            def tile_load(b, i, j):
                if j == 0:
                    alone(sp, (scattered[i], turns(16 * TOPK * K, b, i) + 16 * TOPK * K), (s["tile_turned"], TILES * b))
                else:
                    after(sp, s["tile_turned"], tile_seen(b, j, NX))
                sp.dma_start(xt[:, j % NX], slots_in[i][j * P:(j + 1) * P, :]).then_inc(tile_loaded[j % NX], 16)

            def tile_down(b, i, j):
                if j == 0:
                    after(sp, s["results_free"], b)
                sp.wait_ge(s["tile_copied"], TILES * b + j + 1)
                sp.dma_start(slots_out[i][j * P:(j + 1) * P, :], ot[:, j % NO]).then_inc(stored[j % NO], 16)

            def combine(b, i):
                alone(sp, (s["out_ready"], b + 1))
                sp.dma_start(x_out[b], mix[:]).then_inc(s["written"], 16)

            for dst, src in ((w_dt[:], w_dt_t), (w_bc[:], w_bc_t), (bias_f[:], biases.rearrange("(p c) -> p c", p=P)),
                             (decay[:], a_log), (gam[:], gamma[:, None]), (bet[:], beta[:, None]),
                             (skip[:], d_param[None, :].to_broadcast([P, D])), (gate[:], gate_w),
                             (gate_bias[:], gate_b[None, :].to_broadcast([P, E]))):
                sp.dma_start(dst, src).then_inc(s["small"], 16)
            sp.wait_ge(s["bias_split"], 5)
            for r in range(3):
                sp.dma_start(bias_rows[r].rearrange("(p c) -> p c", p=P), bias_parts[:, r]).then_inc(s["bias_out"], 16)
            sp.wait_ge(s["bias_out"], 48)
            sp.dma_start(bias[:], bias_rows).then_inc(s["bias_in"], 16)
            for e in range(2):
                sp.dma_start(w1_f[:, e], w1[e]).then_inc(w1_loaded[e], 16)
            sp.dma_start(w2_f[:].rearrange("p (e c d) -> p e c d", e=E, c=HC),
                         w2.rearrange("e (c p) d -> p e c d", p=P)).then_inc(s["w_ld"], 16)
            sp.wait_ge(s["zero_set"], 1)
            sp.dma_start(mix[:, 0, 0:E], zeros[:, 0:E]).then_inc(s["written"], 16)
            for i in range(2):
                sp.dma_start(slots_in[i].rearrange("(j p) d -> p j d", p=P),
                             zeros[:, None, :].to_broadcast([P, TILES, D])).then_inc(s["zeroed"], 16)
            walk(sp, dict(load=load, reload=reload, weights=weights, split=split, tile_load=tile_load, tile_down=tile_down, combine=combine))
            sp.wait_ge(s["written"], 16 * (SEQS + 1))

        @block.gpsimd
        def _(pool):
            def weigh(b, i, r):
                n = UNITS * b + r
                pool.wait_ge(s["scanned"], n + 1)
                if r == 0:
                    pool.wait_ge(s["c_ready"], b + 1)
                after(pool, s["reduced"], n - NU + 1)
                nc.gpsimd.tensor_tensor(ch[:, r % NU], hs[:, r % NU], c_rep[:, i], ALU.mult).then_inc(s["weighed"], 1)

            def scatter(b, i, q0, q1):
                if q0 == 0:
                    alone(pool, (s["routed"], b + 1), (s["zeroed"], 16 * 2),
                          *((loaded, 16 * TILES // NX * (b - 1)) for loaded in tile_loaded))
                for q in range(q0, q1):
                    nc.gpsimd.indirect_dma_start(
                        out=slots_in[i], out_offset=bass.IndirectOffsetOnAxis(pos[:, i, q:q + 1], 0),
                        in_=x2[:, i, q % K, :], in_offset=None).then_inc(scattered[i], 16)

            def gather(b, i, q0, q1):
                if q0 == 0:
                    alone(pool, (s["results_free"], b + 1), *((done, 16 * TILES // NO * (b + 1)) for done in stored))
                for q in range(q0, q1):
                    nc.gpsimd.indirect_dma_start(
                        out=yg[:, q // K, q % K, :], out_offset=None, in_=slots_out[i],
                        in_offset=bass.IndirectOffsetOnAxis(pos[:, i, q:q + 1], 0)).then_inc(gathered[i], 16)

            nc.gpsimd.memset(ident[:], 0.0)
            nc.gpsimd.memset(spread_f[:], 0.0)
            nc.gpsimd.memset(fold_f[:], 0.0)
            nc.gpsimd.memset(before[:], 1.0)
            nc.gpsimd.iota(iota_i[:], pattern=[[0, K], [1, E]], base=0, channel_multiplier=0)
            nc.gpsimd.iota(iota_k[:], pattern=[[0, E], [1, K]], base=0, channel_multiplier=0)
            nc.gpsimd.iota(iota_ji[:], pattern=[[1, TILES], [0, E]], base=0, channel_multiplier=0).then_inc(s["pool_set"], 1)
            pool.wait_ge(s["pool_set"], 1)
            nc.gpsimd.affine_select(out=ident[:], in_=ident[:], compare_op=ALU.not_equal, fill=1.0, base=0,
                                    pattern=[[-1, P]], channel_multiplier=1)
            nc.gpsimd.affine_select(out=before[:], in_=before[:], compare_op=ALU.is_gt, fill=0.0, base=0,
                                    pattern=[[1, P]], channel_multiplier=-1)
            nc.gpsimd.affine_select(out=fold_f[:], in_=fold_f[:], compare_op=ALU.not_equal, fill=1.0, base=0,
                                    pattern=[[-J, N], [-1, J]], channel_multiplier=1)
            nc.gpsimd.affine_select(out=spread_f[:], in_=spread_f[:], compare_op=ALU.not_equal, fill=1.0, base=0,
                                    pattern=[[-J, J], [0, N], [-1, J]], channel_multiplier=1).then_inc(s["pool_set"], 1)
            pool.wait_ge(s["pool_set"], 2)
            nc.gpsimd.affine_select(out=spread_f[:], in_=spread_f[:], compare_op=ALU.not_equal, fill=1.0, base=-64,
                                    pattern=[[-J, J], [0, N], [-1, J]], channel_multiplier=1).then_inc(s["pool_set"], 1)
            walk(pool, dict(weigh=weigh, scatter=scatter, gather=gather))

        @block.scalar
        def _(act):
            def rsqrt(src, logs, dst, log_sem, done, n, scale=1.0, col=0):
                nc.scalar.activation(logs, src, ACT.Ln, bias=eps[:, col:col + 1], scale=scale).then_inc(log_sem, 1)
                act.wait_ge(log_sem, n)
                nc.scalar.activation(dst, logs, ACT.Exp, scale=-0.5).then_inc(done, 1)

            def stats(b, i):
                act.wait_ge(s["moments"], b + 1)
                nc.scalar.activation(lv[:, 0], mv[:, i, :, 1], ACT.Ln, bias=eps[:, 0:1])
                nc.scalar.activation(lv[:, 1], mv[:, i, :, 1], ACT.Ln, bias=eps[:, 1:2], scale=1.0 + EPS).then_inc(s["logs"], 1)
                act.wait_ge(s["logs"], b + 1)
                nc.scalar.activation(rs[:, i], lv[:], ACT.Exp, scale=-0.5).then_inc(s["scales"], 1)

            def turn_x(b, i):
                act.wait_ge(s["turned"], b + 1)
                nc.scalar.activation(xa[:, i], misc[:], ACT.Identity, bias=bet[:, 0:1], scale=gam[:, 0:1]).then_inc(s["xa_ready"], 1)

            def states(b, i):
                act.wait_ge(s["b_ps"], b + 1)
                nc.scalar.activation(b_rep[:, i], misc[:], ACT.Copy).then_inc(s["b_ready"], 1)

            def readout(b, i):
                act.wait_ge(s["c_ps"], b + 1)
                nc.scalar.activation(c_rep[:, i], misc[:], ACT.Copy).then_inc(s["c_ready"], 1)

            def delta(b, i):
                act.wait_ge(s["z_ps"], b + 1)
                nc.scalar.activation(sp_l[:], misc[:], ACT.Abs).then_inc(s["sp_abs"], 1)
                act.wait_ge(s["sp_abs"], b + 1)
                nc.scalar.activation(sp_l[:], sp_l[:], ACT.Exp, scale=-1.0).then_inc(s["sp_exp"], 1)
                act.wait_ge(s["sp_exp"], b + 1)
                nc.scalar.activation(sp_l[:], sp_l[:], ACT.Ln, bias=ones[:, 0:1]).then_inc(s["sp_log"], 1)

            def split(b, i):
                act.wait_ge(s["dt_ready"], b + 1)
                after(act, stacked[1 - i], 64 * (b - 1 + i) if i == 0 else 64 * (b + 1))
                nc.scalar.activation(dt_hi[:], dt[:], ACT.Copy).then_inc(s["dt_hi_ready"], 1)
                act.wait_ge(s["gx_ready"], b + 1)
                nc.scalar.activation(gx_hi[:], gx[:], ACT.Copy).then_inc(s["gx_hi_ready"], 1)

            def decay_(b, i, r):
                n = UNITS * b + r
                act.wait_ge(s["dt_rep"], n + 1)
                after(act, s["scanned"], n - 1)
                nc.scalar.activation(ab[:, r % 2], dt_ps[:], ACT.Exp, scale=decay[:, r:r + 1]).then_inc(s["decayed"], 1)

            def weights(b, i, c):
                act.wait_ge(w1_loaded[c % 2], 16 * (c // 2 + 1))
                nc.scalar.activation(w_hi[:, c * HID:(c + 1) * HID], w1_f[:, c % 2], ACT.Copy).then_inc(s["w_split_hi"], 1)

            def y_sum(b, i):
                act.wait_ge(s["y_mom"], b + 1)
                rsqrt(mv_y[:, :, 1], lv_y[:], rs_y[:], s["y_log"], s["y_scale"], b + 1)

            def y_norm(b, i):
                act.wait_ge(s["x1_mom"], b + 1)
                rsqrt(mv_1[:, :, 1], lv_1[:], rs_1[:], s["x1_log"], s["x1_scale"], b + 1)

            def gate_turn(b, i):
                act.wait_ge(s["x2_turned"], b + 1)
                nc.scalar.activation(x2_t[:], misc[:], ACT.Copy).then_inc(s["x2_copied"], 1)

            def route(b, i):
                act.wait_ge(s["route_max"], b + 1)
                nc.scalar.activation(r_exp[:], r_sub[:], ACT.Exp).then_inc(s["route_exp"], 1)

            def tile_turn(b, i, j):
                act.wait_ge(s["tile_turned"], TILES * b + j + 1)
                after(act, s["tile_hid"], TILES * b + j if j == 0 else TILES * b + j - 1)
                nc.scalar.activation(xt_hi[:, j % 2], turn[:, 0:P], ACT.Copy).then_inc(s["tile_hi"], 1)

            def tile_up(b, i, j):
                act.wait_ge(s["tile_hid"], TILES * b + j + 1)
                after(act, s["tile_folded"], TILES * b + j if j == 0 else TILES * b + j - 1)
                nc.scalar.activation(hid[:, j % 2], hid_ps[:], ACT.Relu).then_inc(s["tile_relu"], 1)

            def tile_fold(b, i, j):
                act.wait_ge(s["tile_folded"], TILES * b + j + 1)
                after(act, s["tile_out"], TILES * b + j if j == 0 else TILES * b + j - 1)
                nc.scalar.activation(hid_t[:, j % 2], fold_ps[:], ACT.Copy).then_inc(s["fold_copied"], 1)

            def combine(b, i):
                act.wait_ge(s["mix_mom"], b + 1)
                rsqrt(mv_m[:, :, 1], lv_m[:], rs_m[:], s["mix_log"], s["mix_scale"], b + 1)

            act.preload_act_table_set("natural_log_exp_and_others")
            act.wait_ge(s["dve_set"], 1)
            act.wait_ge(s["small"], 16 * 9)
            nc.scalar.activation(decay[:], decay[:], ACT.Exp).then_inc(s["decay_exp"], 1)
            act.wait_ge(s["decay_set"], 1)
            walk(act, dict(stats=stats, turn=turn_x, states=states, readout=readout, delta=delta, split=split, decay=decay_,
                           weights=weights, y_sum=y_sum, y_norm=y_norm, gate_turn=gate_turn, route=route,
                           tile_turn=tile_turn, tile_up=tile_up, tile_fold=tile_fold, combine=combine))

        @block.vector
        def _(dve):
            def moments(src, st_, mv_, n_tiles, st_sem, mv_sem, n):
                for k in range(n_tiles):
                    last = nc.vector.bn_stats(out=st_[:, k, :], in_=src(k))
                last.then_inc(st_sem, 1)
                alone(dve, (st_sem, n))
                for k in range(n_tiles):
                    last = nc.vector.bn_aggr(out=mv_[:, k, :], in_=st_[:, k, :])
                last.then_inc(mv_sem, 1)

            def stats(b, i):
                alone(dve, (x_loaded[i], turns(16, b, i) + 16))
                moments(lambda k: xs[:, i, k, :], st, mv[:, i], K, s["stats"], s["moments"], b + 1)

            def norm(b, i):
                dve.wait_ge(s["scales"], b + 1)
                after(dve, s["turned"], b - 1)
                for k in range(K):
                    last = nc.vector.tensor_scalar(xn[:, i, k], xs[:, i, k], mv[:, i, k, 0:1], rs[:, i, 1, k:k + 1],
                                                   ALU.subtract, ALU.mult)
                last.then_inc(s["normed"], 1)
                for k in range(K):
                    last = nc.vector.tensor_scalar(u_t[:, i, k], xs[:, i, k], mv[:, i, k, 0:1], rs[:, i, 0, k:k + 1],
                                                   ALU.subtract, ALU.mult)
                last.then_inc(s["skip_ready"], 1)
                dve.wait_ge(s["skip_ready"], 2 * b + 1)
                nc.vector.tensor_tensor(u_t[:, i], u_t[:, i], skip[:, None, :].to_broadcast([P, K, D]),
                                        ALU.mult).then_inc(s["skip_ready"], 1)

            def delta(b, i):
                dve.wait_ge(s["sp_log"], b + 1)
                nc.vector.scalar_tensor_tensor(out=dt[:], in0=misc[:], scalar=0.0, in1=sp_l[:], op0=ALU.max,
                                               op1=ALU.add).then_inc(s["dt_ready"], 1)
                dve.wait_ge(s["dt_ready"], b + 1)
                nc.vector.tensor_tensor(gx[:], dt[:], xa[:, i], ALU.mult).then_inc(s["gx_ready"], 1)

            def split(b, i):
                dve.wait_ge(s["dt_hi_ready"], b + 1)
                nc.vector.tensor_tensor(dt_lo[:], dt[:], dt_hi[:].bitcast(F32), ALU.subtract).then_inc(s["dt_lo_ready"], 1)
                dve.wait_ge(s["gx_hi_ready"], b + 1)
                nc.vector.tensor_tensor(gx_lo[:], gx[:], gx_hi[:].bitcast(F32), ALU.subtract).then_inc(s["gx_lo_ready"], 1)

            def drive(b, i, r):
                n = UNITS * b + r
                if r == 0:
                    dve.wait_ge(s["b_ready"], b + 1)
                dve.wait_ge(s["gx_rep"], n + 1)
                after(dve, s["scanned"], n - 1)
                nc.vector.tensor_tensor(bx[:, r % 2], gx_ps[:], b_rep[:, i], ALU.mult).then_inc(s["driven"], 1)

            def scan(b, i, r):
                n = UNITS * b + r
                dve.wait_ge(s["decayed"], n + 1)
                dve.wait_ge(s["driven"], n + 1)
                after(dve, s["weighed"], n - NU + 1)
                nc.vector.tensor_tensor_scan(hs[:, r % NU], ab[:, r % 2], bx[:, r % 2], 0.0, ALU.mult,
                                             ALU.add).then_inc(s["scanned"], 1)

            def weights(b, i, c):
                cols = slice(c * HID, (c + 1) * HID)
                dve.wait_ge(s["w_split_hi"], c + 1)
                nc.vector.tensor_tensor(w_lo[:, cols], w1_f[:, c % 2], w_hi[:, cols].bitcast(F32),
                                        ALU.subtract).then_inc(s["w_split_lo"], 1)

            def y_sum(b, i):
                dve.wait_ge(s["reduced"], UNITS * (b + 1))
                dve.wait_ge(s["skip_ready"], 2 * b + 2)
                nc.vector.tensor_tensor(y[:], y_ps[:].rearrange("p (k d) -> p k d", k=K), u_t[:, i],
                                        ALU.add).then_inc(s["y_ready"], 1)
                alone(dve, (s["y_ready"], b + 1))
                moments(lambda k: y[:, k, :], st_y, mv_y, K, s["y_stats"], s["y_mom"], b + 1)

            def y_norm(b, i):
                dve.wait_ge(s["y_scale"], b + 1)
                for k in range(K):
                    last = nc.vector.tensor_scalar(y[:, k], y[:, k], mv_y[:, k, 0:1], rs_y[:, k:k + 1],
                                                   ALU.subtract, ALU.mult)
                last.then_inc(s["y_normed"], 1)
                dve.wait_ge(s["y_normed"], b + 1)
                dve.wait_ge(s["x_reloaded"], 16 * (b + 1))
                nc.vector.tensor_tensor(x1[:, bass.ds(K * b, K), :], y[:], xr[:], ALU.add).then_inc(s["x1_ready"], 1)
                alone(dve, (s["x1_ready"], b + 1))
                moments(lambda k: x1[:, bass.ds(K * b + k, 1), :], st_1, mv_1, K, s["x1_stats"], s["x1_mom"], b + 1)

            def x1_norm(b, i):
                dve.wait_ge(s["x1_scale"], b + 1)
                after(dve, scattered[i], turns(16 * TOPK * K, b, i))
                after(dve, s["x2_turned"], b - 1)
                for k in range(K):
                    last = nc.vector.tensor_scalar(x2[:, i, k], x1[:, bass.ds(K * b + k, 1), :], mv_1[:, k, 0:1],
                                                   rs_1[:, k:k + 1], ALU.subtract, ALU.mult)
                last.then_inc(s["x2_ready"], 1)

            def gate_logits(b, i):
                dve.wait_ge(s["logits_ps"], b + 1)
                nc.vector.tensor_tensor(logit[:], misc[:, 0:K * E].rearrange("p (k e) -> p k e", k=K),
                                        gate_bias[:, None, :].to_broadcast([P, K, E]), ALU.add).then_inc(s["logits_ready"], 1)

            def route(b, i):
                def by_tile(a):
                    return a[:, :, None].to_broadcast([P, K, E])
                link = chain(dve, s["route_chain"], ROUTE_LINKS, b)
                dve.wait_ge(s["logits_ready"], b + 1)
                after(dve, gathered[i], turns(16 * TOPK * K, b, i))
                link(nc.vector.tensor_reduce(r_max[:], logit[:], AX.X, ALU.max))
                nc.vector.tensor_tensor(r_sub[:], logit[:], by_tile(r_max), ALU.subtract).then_inc(s["route_max"], 1)
                dve.wait_ge(s["route_exp"], b + 1)
                link(nc.vector.tensor_reduce(r_sum[:], r_exp[:], AX.X, ALU.add))
                link(nc.vector.reciprocal(r_sum[:], r_sum[:]))
                link(nc.vector.tensor_tensor(prob[:], r_exp[:], by_tile(r_sum), ALU.mult))
                p = prob
                for c in range(TOPK):
                    link(nc.vector.tensor_reduce(weight[:, i, c], p[:], AX.X, ALU.max))
                    link(nc.vector.tensor_tensor(eq[:], p[:], by_tile(weight[:, i, c]), ALU.is_equal))
                    link(nc.vector.scalar_tensor_tensor(out=cand[:], in0=eq[:], scalar=-float(E), in1=iota_e[:],
                                                        op0=ALU.mult, op1=ALU.add))
                    link(nc.vector.tensor_reduce(pick[:], cand[:], AX.X, ALU.min))
                    link(nc.vector.tensor_tensor(hot[:, c], cand[:], by_tile(pick), ALU.is_equal))
                    if c == 0:
                        link(nc.vector.scalar_tensor_tensor(out=prob_2[:], in0=hot[:, 0], scalar=-2.0, in1=prob[:],
                                                            op0=ALU.mult, op1=ALU.add))
                        p = prob_2
                nc.vector.tensor_tensor(mask[:], hot[:, 0], hot[:, 1], ALU.add).then_inc(s["mask_ready"], 1)
                dve.wait_ge(s["prefix_ready"], b + 1)
                link(nc.vector.tensor_copy(tot[:], misc[:, K * E:2 * K * E].rearrange("p (k e) -> p e k", k=K)))
                link(nc.vector.tensor_tensor_scan(run[:].rearrange("p e k -> p (e k)"), restart[:].rearrange("p e k -> p (e k)"),
                                                  tot[:].rearrange("p e k -> p (e k)"), 0.0, ALU.mult, ALU.add))
                link(nc.vector.tensor_scalar(cnt_i[:], run[:, :, K - 1], float(P - 1), None, ALU.add))
                link(nc.vector.tensor_scalar(til_i[:], cnt_i[:], 7, None, ALU.logical_shift_right))
                link(nc.vector.tensor_copy(til[:], til_i[:]))
                link(nc.vector.tensor_tensor_scan(end[:], ones[:, 0:E], til[:], 0.0, ALU.mult, ALU.add))
                link(nc.vector.tensor_tensor(beg[:], end[:], til[:], ALU.subtract))
                link(nc.vector.scalar_tensor_tensor(out=pos_a[:], in0=beg[:, :, None].to_broadcast([P, E, K]),
                                                    scalar=float(P), in1=run[:], op0=ALU.mult, op1=ALU.add))
                link(nc.vector.tensor_tensor(pos_b[:], pos_a[:], tot[:], ALU.subtract))
                nc.vector.tensor_tensor(pos_e[:], misc[:, 0:K * E].rearrange("p (k e) -> p k e", k=K),
                                        pos_b[:].rearrange("p e k -> p k e"), ALU.add).then_inc(s["prefix_used"], 1)
                dve.wait_ge(s["prefix_used"], b + 1)
                for c in range(TOPK):
                    last = nc.vector.tensor_tensor(pos_h[:, c * K:(c + 1) * K], hot[:, c], pos_e[:], ALU.mult)
                link(last)
                link(nc.vector.tensor_reduce(pos_f[:], pos_h[:], AX.X, ALU.add))
                nc.vector.tensor_copy(pos[:, i], pos_f[:])
                link(nc.vector.tensor_tensor(past[:], iota_j[:], end[0:1, None, :].to_broadcast([1, TILES, E]), ALU.is_ge))
                link(nc.vector.tensor_reduce(exp_f[:], past[:], AX.X, ALU.add))
                after(dve, s["tile_out"], TILES * (b - 1))
                nc.vector.tensor_scalar(expert[:, i], exp_f[:], float(E - 1), None, ALU.min).then_inc(s["routed"], 1)

            def tile_turn(b, i, j):
                dve.wait_ge(s["tile_hi"], TILES * b + j + 1)
                nc.vector.tensor_tensor(xt_lo[:, j % 2], turn[:, 0:P], xt_hi[:, j % 2].bitcast(F32),
                                        ALU.subtract).then_inc(s["tile_lo"], 1)

            def tile_down(b, i, j):
                dve.wait_ge(s["tile_out"], TILES * b + j + 1)
                after(dve, stored[j % NO], 16 * (TILES // NO * b + j // NO))
                nc.vector.tensor_copy(ot[:, j % NO], out_ps[:, 0:D]).then_inc(s["tile_copied"], 1)

            def combine(b, i):
                dve.wait_ge(gathered[i], turns(16 * TOPK * K, b, i) + 16 * TOPK * K)
                after(dve, s["written"], 16 * (b + 1))
                for k in range(K):
                    last = nc.vector.tensor_scalar(mix[:, k], yg[:, 0, k], weight[:, i, 0, k:k + 1], None, ALU.mult)
                last.then_inc(s["mix_half"], 1)
                dve.wait_ge(s["mix_half"], b + 1)
                for k in range(K):
                    last = nc.vector.scalar_tensor_tensor(out=mix[:, k], in0=yg[:, 1, k], scalar=weight[:, i, 1, k:k + 1],
                                                          in1=mix[:, k], op0=ALU.mult, op1=ALU.add)
                last.then_inc(s["mix_ready"], 1)
                alone(dve, (s["mix_ready"], b + 1))
                moments(lambda k: mix[:, k, :], st_m, mv_m, K, s["mix_stats"], s["mix_mom"], b + 1)
                dve.wait_ge(s["mix_scale"], b + 1)
                for k in range(K):
                    last = nc.vector.tensor_scalar(mix[:, k], mix[:, k], mv_m[:, k, 0:1], rs_m[:, k:k + 1],
                                                   ALU.subtract, ALU.mult)
                last.then_inc(s["results_free"], 1)
                dve.wait_ge(s["results_free"], b + 2)
                nc.vector.tensor_tensor(mix[:], mix[:], x1[:, bass.ds(K * b, K), :], ALU.add).then_inc(s["out_ready"], 1)

            nc.vector.memset(eps[:, 0:1], EPS)
            nc.vector.memset(eps[:, 1:2], EPS * EPS)
            nc.vector.memset(zeros[:], 0.0).then_inc(s["zero_set"], 1)
            nc.vector.memset(ones_b[:], 1.0).then_inc(s["results_free"], 1)
            nc.vector.memset(ones[:], 1.0).then_inc(s["dve_set"], 1)
            dve.wait_ge(s["small"], 16 * 9)
            nc.vector.tensor_copy(bias_parts[:, 0], bias_f[:]).then_inc(s["bias_split"], 1)
            dve.wait_ge(s["bias_split"], 1)
            nc.vector.tensor_tensor(bias_r[:], bias_f[:], bias_parts[:, 0], ALU.subtract).then_inc(s["bias_split"], 1)
            dve.wait_ge(s["bias_split"], 2)
            nc.vector.tensor_copy(bias_parts[:, 1], bias_r[:]).then_inc(s["bias_split"], 1)
            dve.wait_ge(s["bias_split"], 3)
            nc.vector.tensor_tensor(bias_s[:], bias_r[:], bias_parts[:, 1], ALU.subtract).then_inc(s["bias_split"], 1)
            dve.wait_ge(s["bias_split"], 4)
            nc.vector.tensor_copy(bias_parts[:, 2], bias_s[:]).then_inc(s["bias_split"], 1)
            nc.vector.tensor_copy(w_rep[:], w_bc[:].rearrange("d (c n) -> d c n", c=2)[:, :, :, None]
                                  .to_broadcast([D, 2, N, J])).then_inc(s["w_rep_set"], 1)
            dve.wait_ge(s["decay_exp"], 1)
            nc.vector.tensor_scalar(decay[:], decay[:], -1.0, None, ALU.mult).then_inc(s["decay_set"], 1)
            dve.wait_ge(s["pool_set"], 3)
            nc.vector.tensor_copy(spread[:], spread_f[:].rearrange("p a n j -> p a (n j)"))
            nc.vector.tensor_reduce(fold[:], fold_f[:].rearrange("p n j -> p j n"), AX.X, ALU.add)
            nc.vector.tensor_copy(iota_e[:], iota_i[:].rearrange("p (k e) -> p k e", k=K))
            nc.vector.tensor_copy(iota_j[:], iota_ji[:].rearrange("p (j e) -> p j e", e=E))
            nc.vector.tensor_scalar(restart[:], iota_k[:].rearrange("p (e k) -> p e k", e=E), 1.0, None,
                                    ALU.min).then_inc(s["consts"], 1)
            walk(dve, dict(stats=stats, norm=norm, delta=delta, split=split, drive=drive, scan=scan, weights=weights,
                           y_sum=y_sum, y_norm=y_norm, x1_norm=x1_norm, gate_logits=gate_logits, route=route,
                           tile_turn=tile_turn, tile_down=tile_down, combine=combine))

        @block.tensor
        def _(pe):
            def turn_x(b, i):
                pe.wait_ge(s["normed"], b + 1)
                after(pe, s["dt_ready"], b)
                after(pe, s["prefix_used"], b - 2)
                for k in range(K):
                    last = nc.tensor.matmul(misc[:, k * P:(k + 1) * P], xn[:, i, k], ident[:], start=True, stop=True,
                                            is_transpose=True)
                last.then_inc(s["turned"], 1)

            def states(b, i):
                pe.wait_ge(s["xa_ready"], b + 1)
                nc.tensor.matmul(misc[:], w_rep[:, 0].rearrange("d n j -> d (n j)"), xa[:, i], start=True,
                                 stop=True).then_inc(s["b_ps"], 1)

            def readout(b, i):
                pe.wait_ge(s["b_ready"], b + 1)
                nc.tensor.matmul(misc[:], w_rep[:, 1].rearrange("d n j -> d (n j)"), xa[:, i], start=True,
                                 stop=True).then_inc(s["c_ps"], 1)

            def delta(b, i):
                pe.wait_ge(s["c_ready"], b + 1)
                nc.tensor.matmul(misc[:], w_dt[:], xa[:, i], start=True, stop=False)
                nc.tensor.matmul(misc[:], bias[:, BDT_AT:BDT_AT + D], ones_b[:], start=False, stop=True).then_inc(s["z_ps"], 1)

            def rep(b, i, r):
                n = UNITS * b + r
                if r == 0:
                    pe.wait_ge(stacked[i], turns(128, b, i) + 128)
                h, m = divmod(r, J)
                after(pe, s["decayed"], n)
                nc.tensor.matmul(dt_ps[:], spread[:, m], dt_s[:, i, h], start=True, stop=True).then_inc(s["dt_rep"], 1)
                after(pe, s["driven"], n)
                nc.tensor.matmul(gx_ps[:], spread[:, m], gx_s[:, i, h], start=True, stop=True).then_inc(s["gx_rep"], 1)

            def reduce(b, i, r):
                n = UNITS * b + r
                pe.wait_ge(s["weighed"], n + 1)
                if r == 0:
                    after(pe, s["y_ready"], b)
                for k in range(K):
                    last = nc.tensor.matmul(y_ps[:, k * D + r * J:k * D + (r + 1) * J],
                                            ch[:, r % NU, k * P:(k + 1) * P], fold[:], start=True, stop=True)
                last.then_inc(s["reduced"], 1)

            def gate_turn(b, i):
                pe.wait_ge(s["x2_ready"], b + 1)
                pe.wait_ge(s["dt_ready"], min(b + 3, SEQS) if isinstance(b, int) else b + 3)
                for k in range(K):
                    last = nc.tensor.matmul(misc[:, k * P:(k + 1) * P], x2[:, i, k], ident[:], start=True, stop=True,
                                            is_transpose=True)
                last.then_inc(s["x2_turned"], 1)

            def gate_logits(b, i):
                pe.wait_ge(s["x2_copied"], b + 1)
                for k in range(K):
                    last = nc.tensor.matmul(misc[:, k * E:(k + 1) * E], x2_t[:, k * P:(k + 1) * P], gate[:], start=True,
                                            stop=True)
                last.then_inc(s["logits_ps"], 1)

            def route(b, i):
                pe.wait_ge(s["mask_ready"], b + 1)
                m = mask[:].rearrange("p k e -> p (k e)")
                nc.tensor.matmul(misc[:, 0:K * E], before[:], m, start=True, stop=True)
                nc.tensor.matmul(misc[:, K * E:2 * K * E], ones[:], m, start=True, stop=True).then_inc(s["prefix_ready"], 1)

            def tile_turn(b, i, j):
                pe.wait_ge(tile_loaded[j % NX], 16 * (TILES // NX * b + j // NX + 1))
                after(pe, s["tile_lo"], TILES * b + j)
                nc.tensor.matmul(turn[:, 0:P], xt[:, j % NX], ident[:], start=True, stop=True,
                                 is_transpose=True).then_inc(s["tile_turned"], 1)

            def tile_up(b, i, j):
                if j == 0:
                    alone(pe, (s["routed"], b + 1), (s["w_split_lo"], E), (s["w_ld"], 16))
                e = pe.value_load(expert[0:1, i, j:j + 1], min_val=0, max_val=E - 1)
                pe.wait_ge(s["tile_lo"], TILES * b + j + 1)
                after(pe, s["tile_relu"], TILES * b + j)
                nc.tensor.matmul(hid_ps[:], ones_b[:, 0:P], bias[:, bass.ds(e * HID, HID)], start=True, stop=False)
                nc.tensor.matmul(hid_ps[:], xt_lo[:, j % 2], w_hi[:, bass.ds(e * HID, HID)], start=False, stop=False)
                nc.tensor.matmul(hid_ps[:], xt_hi[:, j % 2], w_lo[:, bass.ds(e * HID, HID)], start=False, stop=False)
                nc.tensor.matmul(hid_ps[:], xt_hi[:, j % 2], w_hi[:, bass.ds(e * HID, HID)], start=False,
                                 stop=True).then_inc(s["tile_hid"], 1)

            def tile_fold(b, i, j):
                pe.wait_ge(s["tile_relu"], TILES * b + j + 1)
                after(pe, s["fold_copied"], TILES * b + j)
                for c in range(HC):
                    last = nc.tensor.matmul(fold_ps[:, c * P:(c + 1) * P], hid[:, j % 2, c * P:(c + 1) * P], ident[:],
                                            start=True, stop=True, is_transpose=True)
                last.then_inc(s["tile_folded"], 1)

            def tile_down(b, i, j):
                e = pe.value_load(expert[0:1, i, j:j + 1], min_val=0, max_val=E - 1)
                pe.wait_ge(s["fold_copied"], TILES * b + j + 1)
                after(pe, s["tile_copied"], TILES * b + j)
                o = out_ps[:, 0:D]
                nc.tensor.matmul(o, ones_b[:, 0:P], bias[:, bass.ds(B2_AT + e * D, D)], start=True, stop=False)
                for c in range(HC):
                    last = nc.tensor.matmul(o, hid_t[:, j % 2, c * P:(c + 1) * P], w2_f[:, bass.ds(e * HC * D + c * D, D)],
                                            start=False, stop=(c == HC - 1))
                last.then_inc(s["tile_out"], 1)

            pe.wait_ge(s["pool_set"], 3)
            pe.wait_ge(s["w_rep_set"], 1)
            pe.wait_ge(s["bias_in"], 16)
            pe.wait_ge(s["consts"], 1)
            walk(pe, dict(turn=turn_x, states=states, readout=readout, delta=delta, rep=rep, reduce=reduce,
                          gate_turn=gate_turn, gate_logits=gate_logits, route=route, tile_turn=tile_turn,
                          tile_up=tile_up, tile_fold=tile_fold, tile_down=tile_down))


def kernel(**inputs):
    import numpy as np
    import concourse.bacc as bacc
    from concourse.bass_utils import run_bass_kernel_spmd

    a = {k: np.asarray(v) for k, v in inputs.items()}
    arrays = {
        "x": a["L0_attn_x"],
        "w_dt_t": a["L0_attn_W_dt"].T,
        "w_bc_t": np.concatenate([a["L0_attn_W_B"], a["L0_attn_W_C"]]).T,
        "biases": np.concatenate([a["L0_ffn_b1"].ravel(), a["L0_ffn_b2"].ravel(), a["L0_attn_b_dt"]]),
        "d_param": a["L0_attn_D_param"],
        "a_log": a["L0_attn_A_log"].reshape(UNITS, J, N).transpose(2, 1, 0).reshape(P, UNITS),
        "gamma": a["L0_attn_gamma"],
        "beta": a["L0_attn_beta"],
        "gate_w": a["L0_ffn_gate_w"],
        "gate_b": a["L0_ffn_gate_b"],
        "w1": a["L0_ffn_w1"],
        "w2": a["L0_ffn_w2"],
    }
    arrays = {k: np.ascontiguousarray(v) for k, v in arrays.items()}
    nc = bacc.Bacc("TRN2", target_bir_lowering=False, num_devices=1)
    args = [nc.dram_tensor(k, v.shape, mybir.dt.from_np(v.dtype), kind="ExternalInput").ap() for k, v in arrays.items()]
    out = nc.dram_tensor("out", (SEQS, T, D), F32, kind="ExternalOutput").ap()
    program(nc, *args, out)
    result = run_bass_kernel_spmd(nc, [arrays], core_ids=[0])
    return result.results[0]["out"]
```

```python
from contextlib import ExitStack

import concourse.bass as bass
from concourse import mybir

F32 = mybir.dt.float32
F32R = mybir.dt.float32r
BF16 = mybir.dt.bfloat16
I32 = mybir.dt.int32
U32 = mybir.dt.uint32
ALU = mybir.AluOpType
ACT = mybir.ActivationFunctionType
AX = mybir.AxisListType

P = 128
EPS = 1e-5
SEQS, T, D, N = 8, 512, 128, 16
E, HID, TOPK = 8, 512, 2
K = T // P
J = P // N
UNITS = D // J
TILES = K * TOPK + E - 1
SLOTS = TILES * P
HC = HID // P
NX = 5
NO = 3
assert TILES % NX == 0 and TILES % NO == 0
TOP_LINKS, SECOND_LINKS, START_LINKS, SLOT_LINKS = 8, 6, 9, 4
NU = 4
NBIAS = E * HID + E * D + D
BC = NBIAS // P
B2_AT, BDT_AT = E * HID, E * HID + E * D


PLAN = (
    ("rep", UNITS, UNITS), ("count", 45, 1), ("drive", UNITS, UNITS), ("scan", UNITS + 1, UNITS), ("y_sum", 35, 1),
    ("weigh", UNITS + 1, UNITS), ("tile_keep", 55, TILES), ("tile_copy", 54, TILES),
    ("tile_turn", 52, TILES), ("tile_load", 50, TILES),
    ("scales", 2, 1), ("y_scale", 36, 1), ("x1_scale", 39, 1), ("channels", 3, 1), ("states_copy", 4, 1),
    ("readout_copy", 5, 1), ("gate_copy", 41, 1),
    ("decay", UNITS, UNITS), ("tile_up", 53, TILES), ("load", 0, 1), ("fill", UNITS, 1), ("weights", UNITS, E),
    ("stats", 1, 1), ("norm", 2, 1), ("softplus", 6, 1), ("dt", 7, 1), ("split", 8, 1), ("rest", 9, 1), ("stack", 10, 1),
    ("reload", 33, 1), ("skip", 4, 1), ("y_norm", 37, 1), ("x1_stats", 38, 1), ("x1_norm", 39, 1),
    ("gate_max", 42, 1), ("gate_exp", 42, 1), ("softmax", 43, 1), ("second", 44, 1),
    ("starts", 45, 1), ("slots", 46, 1), ("mix", 76, 1), ("mix_stats", 77, 1), ("mix_scale", 78, 1), ("result", 79, 1),
    ("tile_down", 54, TILES), ("reduce", UNITS + 3, UNITS),
    ("turn", 2, 1), ("states", 3, 1), ("readout", 4, 1), ("delta", 5, 1), ("gate_turn", 40, 1), ("gate_logits", 41, 1),
    ("tile_pick", 52, TILES), ("tile_fold", 53, TILES),
    ("scatter", 46, 4), ("gather", 70, 4),
)
ONCE = ("fill", "weights")
LAST_LAG = max(at + times - 1 for _, at, times in PLAN) // UNITS


def order():
    return [(kind, half - (at + r) // UNITS, r) for half in (0, 1) for u in range(UNITS)
            for kind, at, times in PLAN for r in range(times) if (at + r) % UNITS == u]


def program(nc, x, w_dt_t, w_bc_t, biases, d_param, a_log, gamma, beta, gate_w, gate_b, w1, w2, out):
    slots_in = [nc.dram_tensor(f"slots_in{i}", [SLOTS, D], F32, kind="Internal").ap() for i in range(2)]
    slots_out = [nc.dram_tensor(f"slots_out{i}", [SLOTS, D], F32, kind="Internal").ap() for i in range(2)]
    bias_rows = nc.dram_tensor("bias_rows", [3, NBIAS], BF16, kind="Internal").ap()
    x_in = x.rearrange("b (k p) d -> b p k d", p=P)
    x_out = out.rearrange("b (k p) d -> b p k d", p=P)

    with ExitStack() as ctx:
        def sb(name, shape, dt=F32):
            return ctx.enter_context(nc.sbuf_tensor(name, shape, dt))

        def bank(name):
            return ctx.enter_context(nc.psum_tensor(name, [P, 512], F32))

        ident = sb("ident", [P, P])
        ones = sb("ones", [P, P])
        before = sb("before", [P, P])
        spread_f = sb("spread_f", [P, J, N, J])
        spread = sb("spread", [P, J, P], F32R)
        fold_f = sb("fold_f", [P, N, J])
        fold = sb("fold", [P, J])
        ones_b = sb("ones_b", [3, 512], BF16)
        iota_i = sb("iota_i", [P, K * E], I32)
        iota_k = sb("iota_k", [P, E * K], I32)
        iota_e = sb("iota_e", [P, K, E])
        restart = sb("restart", [P, E, K])
        iota_ji = sb("iota_ji", [1, TILES * E], I32)
        iota_j = sb("iota_j", [1, TILES, E])
        eps = sb("eps", [P, 2])
        w_dt = sb("w_dt", [D, D])
        w_bc = sb("w_bc", [D, 2 * N])
        w_rep = sb("w_rep", [D, 2, N, J])
        decay = sb("decay", [P, UNITS])
        gam = sb("gam", [D, 1])
        bet = sb("bet", [D, 1])
        skip = sb("skip", [P, D])
        gate = sb("gate", [D, E])
        gate_bias = sb("gate_bias", [P, E])
        bias_f = sb("bias_f", [P, BC])
        bias_r = sb("bias_r", [P, BC])
        bias_s = sb("bias_s", [P, BC])
        bias_parts = sb("bias_parts", [P, 3, BC], BF16)
        bias = sb("bias", [3, NBIAS], BF16)
        w1_f = sb("w1_f", [P, 2, HID])
        w2_f = sb("w2_f", [P, E * HC * D])
        w_hi = sb("w_hi", [P, E * HID], F32R)
        w_lo = sb("w_lo", [P, E * HID], F32R)
        zeros = sb("zeros", [P, D])

        xs = sb("xs", [P, 2, K, D])
        xr = sb("xr", [P, K, D])
        st = sb("st", [P, K, 6])
        mv = sb("mv", [P, 2, K, 2])
        lv = sb("lv", [P, 2, K])
        rs = sb("rs", [P, 2, 2, K])
        u_t = sb("u_t", [P, 2, K, D])
        xn = sb("xn", [P, 2, K, D])
        xa = sb("xa", [D, 2, T])
        sp_l = sb("sp_l", [D, T])
        dt = sb("dt", [D, T])
        gx = sb("gx", [D, T])
        dt_hi = sb("dt_hi", [D, T], F32R)
        dt_lo = sb("dt_lo", [D, T], F32R)
        gx_hi = sb("gx_hi", [D, T], F32R)
        gx_lo = sb("gx_lo", [D, T], F32R)
        dt_s = sb("dt_s", [P, 2, 2, T], F32R)
        gx_s = sb("gx_s", [P, 2, 2, T], F32R)
        b_rep = sb("b_rep", [P, 2, T])
        c_rep = sb("c_rep", [P, 2, T])
        ab = sb("ab", [P, 2, T])
        bx = sb("bx", [P, 2, T])
        hs = sb("hs", [P, NU, T])
        ch = sb("ch", [P, NU, T])
        y = sb("y", [P, K, D])
        st_y = sb("st_y", [P, K, 6])
        mv_y = sb("mv_y", [P, K, 2])
        lv_y = sb("lv_y", [P, K])
        rs_y = sb("rs_y", [P, K])
        st_1 = sb("st_1", [P, K, 6])
        mv_1 = sb("mv_1", [P, K, 2])
        lv_1 = sb("lv_1", [P, K])
        rs_1 = sb("rs_1", [P, K])
        x1 = sb("x1", [P, SEQS * K, D])
        x2 = sb("x2", [P, 2, K, D])
        x2_t = sb("x2_t", [D, T])
        logit = sb("logit", [P, K, E])
        r_max = sb("r_max", [P, K])
        r_sub = sb("r_sub", [P, K, E])
        r_exp = sb("r_exp", [P, K, E])
        r_sum = sb("r_sum", [P, K])
        prob = sb("prob", [P, K, E])
        eq = sb("eq", [P, K, E])
        cand = sb("cand", [P, K, E])
        pick = sb("pick", [P, K])
        best = sb("best", [P, TOPK, K])
        hot = sb("hot", [P, TOPK, K, E])
        prob_2 = sb("prob_2", [P, K, E])
        mask = sb("mask", [P, K, E])
        tot = sb("tot", [P, E, K])
        run = sb("run", [P, E, K])
        cnt_i = sb("cnt_i", [P, E], I32)
        til_i = sb("til_i", [P, E], I32)
        til = sb("til", [P, E])
        end = sb("end", [P, E])
        beg = sb("beg", [P, E])
        pos_a = sb("pos_a", [P, E, K])
        pos_b = sb("pos_b", [P, E, K])
        pos_e = sb("pos_e", [P, K, E])
        pos_h = sb("pos_h", [P, TOPK * K, E])
        pos_f = sb("pos_f", [P, TOPK * K])
        pos = sb("pos", [P, 2, TOPK * K], U32)
        weight = sb("weight", [P, 2, TOPK, K])
        past = sb("past", [1, TILES, E])
        exp_f = sb("exp_f", [1, TILES])
        expert = sb("expert", [1, 2, TILES], I32)
        xt = sb("xt", [P, NX, D])
        xt_hi = sb("xt_hi", [D, 2, P], F32R)
        xt_lo = sb("xt_lo", [D, 2, P], F32R)
        hid = sb("hid", [P, 2, HID])
        hid_t = sb("hid_t", [P, 2, HID])
        ot = sb("ot", [P, NO, D])
        yg = sb("yg", [P, TOPK, K, D])
        mix = sb("mix", [P, K, D])
        st_m = sb("st_m", [P, K, 6])
        mv_m = sb("mv_m", [P, K, 2])
        lv_m = sb("lv_m", [P, K])
        rs_m = sb("rs_m", [P, K])

        dt_ps = bank("dt_ps")
        gx_ps = bank("gx_ps")
        y_ps = bank("y_ps")
        misc = bank("misc")
        turn = bank("turn")
        out_ps = bank("out_ps")
        hid_ps = bank("hid_ps")
        fold_ps = bank("fold_ps")

        names = """consts results_free pool_set mix_half route_done prefix_used dve_set small bias_ld bias_split bias_out bias_in w_ld w_split_hi w_split_lo w_rep_set
            decay_exp decay_set zero_set zeroed iota_set
            stats moments logs scales normed turned xa_ready b_ps b_ready c_ps c_ready z_ps sp_abs sp_exp sp_log
            dt_ready gx_ready dt_hi_ready gx_hi_ready dt_lo_ready gx_lo_ready
            dt_rep gx_rep decayed driven scanned weighed reduced
            skip_ready y_ready y_stats y_mom y_log y_scale y_normed x1_ready x1_stats x1_mom x1_log x1_scale x2_ready
            x_reloaded x2_turned x2_copied logits_ps logits_ready max_ready top_chain second_chain start_chain slot_chain route_max route_exp mask_ready prefix_ready routed
            tile_turned tile_hi tile_lo tile_hid tile_relu tile_folded fold_copied tile_out tile_copied
            mix_ready mix_stats mix_mom mix_log mix_scale out_ready written""".split()
        s = {n: ctx.enter_context(nc.semaphore(n)) for n in names}
        x_loaded = [ctx.enter_context(nc.semaphore(f"x_loaded{i}")) for i in range(2)]
        tile_loaded = [ctx.enter_context(nc.semaphore(f"tile_loaded{i}")) for i in range(NX)]
        stacked = [ctx.enter_context(nc.semaphore(f"stacked{i}")) for i in range(2)]
        scattered = [ctx.enter_context(nc.semaphore(f"scattered{i}")) for i in range(2)]
        gathered = [ctx.enter_context(nc.semaphore(f"gathered{i}")) for i in range(2)]
        w1_loaded = [ctx.enter_context(nc.semaphore(f"w1_loaded{i}")) for i in range(2)]
        stored = [ctx.enter_context(nc.semaphore(f"stored{i}")) for i in range(NO)]
        steps = order()

        def after(eng, sem, n):
            if not (isinstance(n, int) and n <= 0):
                eng.wait_ge(sem, n)

        def alone(eng, *waits):
            for _, n in waits:
                if not isinstance(n, int):
                    eng.compute_val(n)
            eng.wait_ge(s["consts"], 1)
            for sem, n in waits:
                after(eng, sem, n)

        def chain(eng, sem, per, index):
            n = [0]

            def link(ins):
                n[0] += 1
                ins.then_inc(sem, 1)
                eng.wait_ge(sem, per * index + n[0])
            return link

        def turns(per, b, i):
            return per // 2 * (b - i)

        def tile_seen(b, j, n):
            return TILES * b + (j - n + 1 if j >= n else 0)

        def walk(eng, parts):
            def iteration(it, first, last):
                if "begin" in parts:
                    parts["begin"]()
                for kind, c, r in steps:
                    if kind in parts and 2 * first + c >= 0 and 2 * last + c < SEQS and (
                            kind not in ONCE or last == 0):
                        parts[kind](2 * it + c, c % 2, r)

            ahead = LAST_LAG // 2
            for it in range(ahead):
                iteration(it, it, it)
            with eng.Fori(ahead, SEQS // 2) as it:
                iteration(it, ahead, SEQS // 2 - 1)
            for it in range(SEQS // 2, SEQS // 2 + ahead):
                iteration(it, it, it)

        block = ctx.enter_context(nc.Block())

        @block.sync
        def _(sp):
            def load(b, i, _):
                if isinstance(b, int) and b == 0:
                    return
                alone(sp, (s["skip_ready"], 2 * b - 3))
                sp.dma_start(xs[:, i], x_in[b]).then_inc(x_loaded[i], 16)

            def reload(b, i, _):
                alone(sp, (s["x1_ready"], b))
                sp.dma_start(xr[:], x_in[b]).then_inc(s["x_reloaded"], 16)

            def weights(b, i, c):
                if c + 2 < E:
                    sp.wait_ge(s["w_split_lo"], c + 1)
                    sp.dma_start(w1_f[:, c % 2], w1[c + 2]).then_inc(w1_loaded[c % 2], 16)

            def fill(b, i, _):
                for e in range(2):
                    sp.dma_start(w1_f[:, e], w1[e]).then_inc(w1_loaded[e], 16)
                sp.dma_start(w2_f[:].rearrange("p (e c d) -> p e c d", e=E, c=HC),
                             w2.rearrange("e (c p) d -> p e c d", p=P)).then_inc(s["w_ld"], 16)
                sp.wait_ge(s["zero_set"], 1)
                sp.dma_start(mix[:, 0, 0:E], zeros[:, 0:E]).then_inc(s["written"], 16)
                for i in range(2):
                    sp.dma_start(slots_in[i].rearrange("(j p) d -> p j d", p=P),
                                 zeros[:, None, :].to_broadcast([P, TILES, D])).then_inc(s["zeroed"], 16)

            def stack(b, i, _):
                if not isinstance(b, int):
                    sp.compute_val(b + 1)
                alone(sp, (s["dt_rep"], UNITS * (b - 1)), (s["gx_rep"], UNITS * (b - 1)))
                for hi, lo, hi_sem, lo_sem, dst in ((dt_hi, dt_lo, s["dt_hi_ready"], s["dt_lo_ready"], dt_s),
                                                    (gx_hi, gx_lo, s["gx_hi_ready"], s["gx_lo_ready"], gx_s)):
                    alone(sp, (hi_sem, b + 1))
                    for h in range(2):
                        sp.dma_start(dst[0:64, i, h].bitcast(F32), hi[64 * h:64 * h + 64, :].bitcast(F32)).then_inc(stacked[i], 16)
                    alone(sp, (lo_sem, b + 1))
                    for h in range(2):
                        sp.dma_start(dst[64:128, i, h].bitcast(F32), lo[64 * h:64 * h + 64, :].bitcast(F32)).then_inc(stacked[i], 16)

            def tile_load(b, i, j):
                if j == 0:
                    alone(sp, (scattered[i], turns(16 * TOPK * K, b, i) + 16 * TOPK * K), (s["tile_turned"], TILES * b))
                else:
                    after(sp, s["tile_turned"], tile_seen(b, j, NX))
                sp.dma_start(xt[:, j % NX], slots_in[i][j * P:(j + 1) * P, :]).then_inc(tile_loaded[j % NX], 16)

            def tile_keep(b, i, j):
                if j == 0:
                    alone(sp, (s["results_free"], b), (s["tile_copied"], TILES * b + j + 1))
                else:
                    sp.wait_ge(s["tile_copied"], TILES * b + j + 1)
                sp.dma_start(slots_out[i][j * P:(j + 1) * P, :], ot[:, j % NO]).then_inc(stored[j % NO], 16)

            def result(b, i, _):
                alone(sp, (s["out_ready"], b + 1))
                sp.dma_start(x_out[b], mix[:]).then_inc(s["written"], 16)

            sp.dma_start(xs[:, 0], x_in[0]).then_inc(x_loaded[0], 16)
            for dst, src in ((bias_f[:], biases.rearrange("(p c) -> p c", p=P)), (w_dt[:], w_dt_t), (w_bc[:], w_bc_t),
                             (decay[:], a_log), (gam[:], gamma[:, None]), (bet[:], beta[:, None]),
                             (skip[:], d_param[None, :].to_broadcast([P, D])), (gate[:], gate_w),
                             (gate_bias[:], gate_b[None, :].to_broadcast([P, E]))):
                sp.dma_start(dst, src).then_inc(s["small"], 16)
            sp.wait_ge(s["bias_split"], 5)
            for r in range(3):
                sp.dma_start(bias_rows[r].rearrange("(p c) -> p c", p=P), bias_parts[:, r]).then_inc(s["bias_out"], 16)
            sp.wait_ge(s["bias_out"], 48)
            sp.dma_start(bias[:], bias_rows).then_inc(s["bias_in"], 16)
            walk(sp, dict(load=load, fill=fill, reload=reload, weights=weights, stack=stack, tile_load=tile_load,
                          tile_keep=tile_keep, result=result))
            sp.wait_ge(s["written"], 16 * (SEQS + 1))

        @block.gpsimd
        def _(pool):
            def weigh(b, i, r):
                n = UNITS * b + r
                pool.wait_ge(s["scanned"], n + 1)
                if r == 0:
                    pool.wait_ge(s["c_ready"], b + 1)
                after(pool, s["reduced"], n - NU + 1)
                nc.gpsimd.tensor_tensor(ch[:, r % NU], hs[:, r % NU], c_rep[:, i], ALU.mult).then_inc(s["weighed"], 1)

            def scatter(b, i, r):
                if r == 0:
                    alone(pool, (s["routed"], b + 1), (s["zeroed"], 16 * 2),
                          *((loaded, 16 * TILES // NX * (b - 1)) for loaded in tile_loaded))
                for q in (2 * r, 2 * r + 1):
                    nc.gpsimd.indirect_dma_start(
                        out=slots_in[i], out_offset=bass.IndirectOffsetOnAxis(pos[:, i, q:q + 1], 0),
                        in_=x2[:, i, q % K, :], in_offset=None).then_inc(scattered[i], 16)

            def gather(b, i, r):
                if r == 0:
                    alone(pool, (s["results_free"], b + 1), *((done, 16 * TILES // NO * (b + 1)) for done in stored))
                for q in (2 * r, 2 * r + 1):
                    nc.gpsimd.indirect_dma_start(
                        out=yg[:, q // K, q % K, :], out_offset=None, in_=slots_out[i],
                        in_offset=bass.IndirectOffsetOnAxis(pos[:, i, q:q + 1], 0)).then_inc(gathered[i], 16)

            def skip_path(b, i, _):
                pool.wait_ge(s["skip_ready"], 2 * b + 1)
                nc.gpsimd.tensor_tensor(u_t[:, i], u_t[:, i], skip[:, None, :].to_broadcast([P, K, D]),
                                        ALU.mult).then_inc(s["skip_ready"], 1)

            def dt_gx(b, i, _):
                pool.wait_ge(s["dt_ready"], b + 1)
                nc.gpsimd.tensor_tensor(gx[:], dt[:], xa[:, i], ALU.mult).then_inc(s["gx_ready"], 1)

            def result(b, i, _):
                pool.wait_ge(s["results_free"], b + 2)
                nc.gpsimd.tensor_tensor(mix[:], mix[:], x1[:, bass.ds(K * b, K), :], ALU.add).then_inc(s["out_ready"], 1)

            nc.gpsimd.memset(ident[:], 0.0)
            nc.gpsimd.memset(spread_f[:], 0.0)
            nc.gpsimd.memset(fold_f[:], 0.0)
            nc.gpsimd.memset(before[:], 1.0)
            nc.gpsimd.iota(iota_i[:], pattern=[[0, K], [1, E]], base=0, channel_multiplier=0)
            nc.gpsimd.iota(iota_k[:], pattern=[[0, E], [1, K]], base=0, channel_multiplier=0)
            nc.gpsimd.iota(iota_ji[:], pattern=[[1, TILES], [0, E]], base=0, channel_multiplier=0).then_inc(s["pool_set"], 1)
            pool.wait_ge(s["pool_set"], 1)
            nc.gpsimd.affine_select(out=ident[:], in_=ident[:], compare_op=ALU.not_equal, fill=1.0, base=0,
                                    pattern=[[-1, P]], channel_multiplier=1)
            nc.gpsimd.affine_select(out=before[:], in_=before[:], compare_op=ALU.is_gt, fill=0.0, base=0,
                                    pattern=[[1, P]], channel_multiplier=-1)
            nc.gpsimd.affine_select(out=fold_f[:], in_=fold_f[:], compare_op=ALU.not_equal, fill=1.0, base=0,
                                    pattern=[[-J, N], [-1, J]], channel_multiplier=1)
            nc.gpsimd.affine_select(out=spread_f[:], in_=spread_f[:], compare_op=ALU.not_equal, fill=1.0, base=0,
                                    pattern=[[-J, J], [0, N], [-1, J]], channel_multiplier=1).then_inc(s["pool_set"], 1)
            pool.wait_ge(s["pool_set"], 2)
            nc.gpsimd.affine_select(out=spread_f[:], in_=spread_f[:], compare_op=ALU.not_equal, fill=1.0, base=-64,
                                    pattern=[[-J, J], [0, N], [-1, J]], channel_multiplier=1).then_inc(s["pool_set"], 1)
            walk(pool, dict(weigh=weigh, skip=skip_path, dt=dt_gx, scatter=scatter, gather=gather, result=result))

        @block.scalar
        def _(act):
            def rsqrt(src, logs, dst, log_sem, done, n, scale=1.0, col=0):
                nc.scalar.activation(logs, src, ACT.Ln, bias=eps[:, col:col + 1], scale=scale).then_inc(log_sem, 1)
                act.wait_ge(log_sem, n)
                nc.scalar.activation(dst, logs, ACT.Exp, scale=-0.5).then_inc(done, 1)

            def scales(b, i, _):
                act.wait_ge(s["moments"], b + 1)
                nc.scalar.activation(lv[:, 0], mv[:, i, :, 1], ACT.Ln, bias=eps[:, 0:1])
                nc.scalar.activation(lv[:, 1], mv[:, i, :, 1], ACT.Ln, bias=eps[:, 1:2], scale=1.0 + EPS).then_inc(s["logs"], 1)
                act.wait_ge(s["logs"], b + 1)
                nc.scalar.activation(rs[:, i], lv[:], ACT.Exp, scale=-0.5).then_inc(s["scales"], 1)

            def channels(b, i, _):
                act.wait_ge(s["turned"], b + 1)
                nc.scalar.activation(xa[:, i], misc[:], ACT.Identity, bias=bet[:, 0:1], scale=gam[:, 0:1]).then_inc(s["xa_ready"], 1)

            def states_copy(b, i, _):
                act.wait_ge(s["b_ps"], b + 1)
                nc.scalar.activation(b_rep[:, i], misc[:], ACT.Copy).then_inc(s["b_ready"], 1)

            def readout_copy(b, i, _):
                act.wait_ge(s["c_ps"], b + 1)
                nc.scalar.activation(c_rep[:, i], misc[:], ACT.Copy).then_inc(s["c_ready"], 1)

            def softplus(b, i, _):
                act.wait_ge(s["z_ps"], b + 1)
                nc.scalar.activation(sp_l[:], misc[:], ACT.Abs).then_inc(s["sp_abs"], 1)
                act.wait_ge(s["sp_abs"], b + 1)
                nc.scalar.activation(sp_l[:], sp_l[:], ACT.Exp, scale=-1.0).then_inc(s["sp_exp"], 1)
                act.wait_ge(s["sp_exp"], b + 1)
                nc.scalar.activation(sp_l[:], sp_l[:], ACT.Ln, bias=ones[:, 0:1]).then_inc(s["sp_log"], 1)

            def split(b, i, _):
                act.wait_ge(s["dt_ready"], b + 1)
                after(act, stacked[1 - i], 64 * (b - 1 + i) if i == 0 else 64 * (b + 1))
                nc.scalar.activation(dt_hi[:], dt[:], ACT.Copy).then_inc(s["dt_hi_ready"], 1)
                act.wait_ge(s["gx_ready"], b + 1)
                nc.scalar.activation(gx_hi[:], gx[:], ACT.Copy).then_inc(s["gx_hi_ready"], 1)

            def decay_(b, i, r):
                n = UNITS * b + r
                act.wait_ge(s["dt_rep"], n + 1)
                after(act, s["scanned"], n - 1)
                nc.scalar.activation(ab[:, r % 2], dt_ps[:], ACT.Exp, scale=decay[:, r:r + 1]).then_inc(s["decayed"], 1)

            def weights(b, i, c):
                act.wait_ge(w1_loaded[c % 2], 16 * (c // 2 + 1))
                nc.scalar.activation(w_hi[:, c * HID:(c + 1) * HID], w1_f[:, c % 2], ACT.Copy).then_inc(s["w_split_hi"], 1)

            def y_scale(b, i, _):
                act.wait_ge(s["y_mom"], b + 1)
                rsqrt(mv_y[:, :, 1], lv_y[:], rs_y[:], s["y_log"], s["y_scale"], b + 1)

            def x1_scale(b, i, _):
                act.wait_ge(s["x1_mom"], b + 1)
                rsqrt(mv_1[:, :, 1], lv_1[:], rs_1[:], s["x1_log"], s["x1_scale"], b + 1)

            def gate_copy(b, i, _):
                act.wait_ge(s["x2_turned"], b + 1)
                nc.scalar.activation(x2_t[:], misc[:], ACT.Copy).then_inc(s["x2_copied"], 1)

            def gate_exp(b, i, _):
                act.wait_ge(s["route_max"], b + 1)
                nc.scalar.activation(r_exp[:], r_sub[:], ACT.Exp).then_inc(s["route_exp"], 1)

            def tile_turn(b, i, j):
                act.wait_ge(s["tile_turned"], TILES * b + j + 1)
                after(act, s["tile_hid"], TILES * b + j - 1)
                nc.scalar.activation(xt_hi[:, (i + j) % 2], turn[:, 0:P], ACT.Copy).then_inc(s["tile_hi"], 1)

            def tile_up(b, i, j):
                act.wait_ge(s["tile_hid"], TILES * b + j + 1)
                after(act, s["tile_folded"], TILES * b + j - 1)
                nc.scalar.activation(hid[:, (i + j) % 2], hid_ps[:], ACT.Relu).then_inc(s["tile_relu"], 1)

            def tile_copy(b, i, j):
                act.wait_ge(s["tile_folded"], TILES * b + j + 1)
                after(act, s["tile_out"], TILES * b + j - 1)
                nc.scalar.activation(hid_t[:, (i + j) % 2], fold_ps[:], ACT.Copy).then_inc(s["fold_copied"], 1)

            def tile_keep(b, i, j):
                act.wait_ge(s["tile_out"], TILES * b + j + 1)
                after(act, stored[j % NO], 16 * (TILES // NO * b + j // NO))
                nc.scalar.activation(ot[:, j % NO], out_ps[:, 0:D], ACT.Copy).then_inc(s["tile_copied"], 1)

            def mix_scale(b, i, _):
                act.wait_ge(s["mix_mom"], b + 1)
                rsqrt(mv_m[:, :, 1], lv_m[:], rs_m[:], s["mix_log"], s["mix_scale"], b + 1)

            act.preload_act_table_set("natural_log_exp_and_others")
            act.wait_ge(s["dve_set"], 1)
            act.wait_ge(s["small"], 16 * 9)
            nc.scalar.activation(decay[:], decay[:], ACT.Exp).then_inc(s["decay_exp"], 1)
            act.wait_ge(s["decay_set"], 1)
            walk(act, dict(scales=scales, channels=channels, states_copy=states_copy, readout_copy=readout_copy,
                           softplus=softplus, split=split, decay=decay_, weights=weights, y_scale=y_scale,
                           x1_scale=x1_scale, gate_copy=gate_copy, gate_exp=gate_exp, tile_turn=tile_turn,
                           tile_up=tile_up, tile_copy=tile_copy, tile_keep=tile_keep, mix_scale=mix_scale))

        @block.vector
        def _(dve):
            def moments(src, st_, mv_, n_tiles, st_sem, mv_sem, n):
                for k in range(n_tiles):
                    last = nc.vector.bn_stats(out=st_[:, k, :], in_=src(k))
                last.then_inc(st_sem, 1)
                alone(dve, (st_sem, n))
                for k in range(n_tiles):
                    last = nc.vector.bn_aggr(out=mv_[:, k, :], in_=st_[:, k, :])
                last.then_inc(mv_sem, 1)

            def stats(b, i, _):
                alone(dve, (x_loaded[i], turns(16, b, i) + 16))
                moments(lambda k: xs[:, i, k, :], st, mv[:, i], K, s["stats"], s["moments"], b + 1)

            def norm(b, i, _):
                dve.wait_ge(s["scales"], b + 1)
                after(dve, s["turned"], b - 1)
                for k in range(K):
                    last = nc.vector.tensor_scalar(xn[:, i, k], xs[:, i, k], mv[:, i, k, 0:1], rs[:, i, 1, k:k + 1],
                                                   ALU.subtract, ALU.mult)
                last.then_inc(s["normed"], 1)

            def skip_path(b, i, _):
                for k in range(K):
                    last = nc.vector.tensor_scalar(u_t[:, i, k], xs[:, i, k], mv[:, i, k, 0:1], rs[:, i, 0, k:k + 1],
                                                   ALU.subtract, ALU.mult)
                last.then_inc(s["skip_ready"], 1)

            def dt_gx(b, i, _):
                dve.wait_ge(s["sp_log"], b + 1)
                nc.vector.scalar_tensor_tensor(out=dt[:], in0=misc[:], scalar=0.0, in1=sp_l[:], op0=ALU.max,
                                               op1=ALU.add).then_inc(s["dt_ready"], 1)

            def rest(b, i, _):
                dve.wait_ge(s["dt_hi_ready"], b + 1)
                nc.vector.tensor_tensor(dt_lo[:], dt[:], dt_hi[:].bitcast(F32), ALU.subtract).then_inc(s["dt_lo_ready"], 1)
                dve.wait_ge(s["gx_hi_ready"], b + 1)
                nc.vector.tensor_tensor(gx_lo[:], gx[:], gx_hi[:].bitcast(F32), ALU.subtract).then_inc(s["gx_lo_ready"], 1)

            def drive(b, i, r):
                n = UNITS * b + r
                if r == 0:
                    dve.wait_ge(s["b_ready"], b + 1)
                dve.wait_ge(s["gx_rep"], n + 1)
                after(dve, s["scanned"], n - 1)
                nc.vector.tensor_tensor(bx[:, r % 2], gx_ps[:], b_rep[:, i], ALU.mult).then_inc(s["driven"], 1)

            def scan(b, i, r):
                n = UNITS * b + r
                dve.wait_ge(s["decayed"], n + 1)
                dve.wait_ge(s["driven"], n + 1)
                after(dve, s["weighed"], n - NU + 1)
                nc.vector.tensor_tensor_scan(hs[:, r % NU], ab[:, r % 2], bx[:, r % 2], 0.0, ALU.mult,
                                             ALU.add).then_inc(s["scanned"], 1)

            def weights(b, i, c):
                cols = slice(c * HID, (c + 1) * HID)
                dve.wait_ge(s["w_split_hi"], c + 1)
                nc.vector.tensor_tensor(w_lo[:, cols], w1_f[:, c % 2], w_hi[:, cols].bitcast(F32),
                                        ALU.subtract).then_inc(s["w_split_lo"], 1)

            def y_sum(b, i, _):
                dve.wait_ge(s["reduced"], UNITS * (b + 1))
                dve.wait_ge(s["skip_ready"], 2 * b + 2)
                nc.vector.tensor_tensor(y[:], y_ps[:].rearrange("p (k d) -> p k d", k=K), u_t[:, i],
                                        ALU.add).then_inc(s["y_ready"], 1)
                alone(dve, (s["y_ready"], b + 1))
                moments(lambda k: y[:, k, :], st_y, mv_y, K, s["y_stats"], s["y_mom"], b + 1)

            def y_norm(b, i, _):
                dve.wait_ge(s["y_scale"], b + 1)
                for k in range(K):
                    last = nc.vector.tensor_scalar(y[:, k], y[:, k], mv_y[:, k, 0:1], rs_y[:, k:k + 1],
                                                   ALU.subtract, ALU.mult)
                last.then_inc(s["y_normed"], 1)
                dve.wait_ge(s["y_normed"], b + 1)
                dve.wait_ge(s["x_reloaded"], 16 * (b + 1))
                nc.vector.tensor_tensor(x1[:, bass.ds(K * b, K), :], y[:], xr[:], ALU.add).then_inc(s["x1_ready"], 1)

            def x1_stats(b, i, _):
                alone(dve, (s["x1_ready"], b + 1))
                moments(lambda k: x1[:, bass.ds(K * b + k, 1), :], st_1, mv_1, K, s["x1_stats"], s["x1_mom"], b + 1)

            def x1_norm(b, i, _):
                dve.wait_ge(s["x1_scale"], b + 1)
                after(dve, scattered[i], turns(16 * TOPK * K, b, i))
                after(dve, s["x2_turned"], b - 1)
                for k in range(K):
                    last = nc.vector.tensor_scalar(x2[:, i, k], x1[:, bass.ds(K * b + k, 1), :], mv_1[:, k, 0:1],
                                                   rs_1[:, k:k + 1], ALU.subtract, ALU.mult)
                last.then_inc(s["x2_ready"], 1)

            def by_tile(a):
                return a[:, :, None].to_broadcast([P, K, E])

            def gate_max(b, i, _):
                dve.wait_ge(s["logits_ps"], b + 1)
                nc.vector.tensor_tensor(logit[:], misc[:, 0:K * E].rearrange("p (k e) -> p k e", k=K),
                                        gate_bias[:, None, :].to_broadcast([P, K, E]), ALU.add).then_inc(s["logits_ready"], 1)
                dve.wait_ge(s["logits_ready"], b + 1)
                nc.vector.tensor_reduce(r_max[:], logit[:], AX.X, ALU.max).then_inc(s["max_ready"], 1)
                dve.wait_ge(s["max_ready"], b + 1)
                nc.vector.tensor_tensor(r_sub[:], logit[:], by_tile(r_max), ALU.subtract).then_inc(s["route_max"], 1)

            def top(link, c, p):
                link(nc.vector.tensor_reduce(best[:, c], p[:], AX.X, ALU.max))
                link(nc.vector.tensor_tensor(eq[:], p[:], by_tile(best[:, c]), ALU.is_equal))
                link(nc.vector.scalar_tensor_tensor(out=cand[:], in0=eq[:], scalar=-float(E), in1=iota_e[:],
                                                    op0=ALU.mult, op1=ALU.add))
                link(nc.vector.tensor_reduce(pick[:], cand[:], AX.X, ALU.min))

            def softmax(b, i, _):
                link = chain(dve, s["top_chain"], TOP_LINKS, b)
                dve.wait_ge(s["route_exp"], b + 1)
                link(nc.vector.tensor_reduce(r_sum[:], r_exp[:], AX.X, ALU.add))
                link(nc.vector.reciprocal(r_sum[:], r_sum[:]))
                link(nc.vector.tensor_tensor(prob[:], r_exp[:], by_tile(r_sum), ALU.mult))
                top(link, 0, prob)
                link(nc.vector.tensor_tensor(hot[:, 0], cand[:], by_tile(pick), ALU.is_equal))

            def second(b, i, _):
                link = chain(dve, s["second_chain"], SECOND_LINKS, b)
                link(nc.vector.scalar_tensor_tensor(out=prob_2[:], in0=hot[:, 0], scalar=-2.0, in1=prob[:],
                                                    op0=ALU.mult, op1=ALU.add))
                top(link, 1, prob_2)
                link(nc.vector.tensor_tensor(hot[:, 1], cand[:], by_tile(pick), ALU.is_equal))
                nc.vector.tensor_tensor(mask[:], hot[:, 0], hot[:, 1], ALU.add).then_inc(s["mask_ready"], 1)

            def starts(b, i, _):
                link = chain(dve, s["start_chain"], START_LINKS, b)
                dve.wait_ge(s["prefix_ready"], b + 1)
                link(nc.vector.tensor_copy(tot[:], misc[:, K * E:2 * K * E].rearrange("p (k e) -> p e k", k=K)))
                link(nc.vector.tensor_tensor_scan(run[:].rearrange("p e k -> p (e k)"), restart[:].rearrange("p e k -> p (e k)"),
                                                  tot[:].rearrange("p e k -> p (e k)"), 0.0, ALU.mult, ALU.add))
                link(nc.vector.tensor_scalar(cnt_i[:], run[:, :, K - 1], float(P - 1), None, ALU.add))
                link(nc.vector.tensor_scalar(til_i[:], cnt_i[:], 7, None, ALU.logical_shift_right))
                link(nc.vector.tensor_copy(til[:], til_i[:]))
                link(nc.vector.tensor_tensor_scan(end[:], ones[:, 0:E], til[:], 0.0, ALU.mult, ALU.add))
                link(nc.vector.tensor_tensor(beg[:], end[:], til[:], ALU.subtract))
                link(nc.vector.scalar_tensor_tensor(out=pos_a[:], in0=beg[:, :, None].to_broadcast([P, E, K]),
                                                    scalar=float(P), in1=run[:], op0=ALU.mult, op1=ALU.add))
                link(nc.vector.tensor_tensor(pos_b[:], pos_a[:], tot[:], ALU.subtract))
                nc.vector.tensor_tensor(pos_e[:], misc[:, 0:K * E].rearrange("p (k e) -> p k e", k=K),
                                        pos_b[:].rearrange("p e k -> p k e"), ALU.add).then_inc(s["prefix_used"], 1)

            def slots(b, i, _):
                link = chain(dve, s["slot_chain"], SLOT_LINKS, b)
                dve.wait_ge(s["prefix_used"], b + 1)
                nc.vector.tensor_copy(weight[:, i], best[:])
                for c in range(TOPK):
                    last = nc.vector.tensor_tensor(pos_h[:, c * K:(c + 1) * K], hot[:, c], pos_e[:], ALU.mult)
                link(last)
                link(nc.vector.tensor_reduce(pos_f[:], pos_h[:], AX.X, ALU.add))
                after(dve, gathered[i], turns(16 * TOPK * K, b, i))
                nc.vector.tensor_copy(pos[:, i], pos_f[:])
                link(nc.vector.tensor_tensor(past[:], iota_j[:], end[0:1, None, :].to_broadcast([1, TILES, E]), ALU.is_ge))
                link(nc.vector.tensor_reduce(exp_f[:], past[:], AX.X, ALU.add))
                after(dve, s["tile_out"], TILES * (b - 1))
                nc.vector.tensor_scalar(expert[:, i], exp_f[:], float(E - 1), None, ALU.min).then_inc(s["routed"], 1)

            def tile_turn(b, i, j):
                dve.wait_ge(s["tile_hi"], TILES * b + j + 1)
                nc.vector.tensor_tensor(xt_lo[:, (i + j) % 2], turn[:, 0:P], xt_hi[:, (i + j) % 2].bitcast(F32),
                                        ALU.subtract).then_inc(s["tile_lo"], 1)

            def mix_results(b, i, _):
                dve.wait_ge(gathered[i], turns(16 * TOPK * K, b, i) + 16 * TOPK * K)
                after(dve, s["written"], 16 * (b + 1))
                for k in range(K):
                    last = nc.vector.tensor_scalar(mix[:, k], yg[:, 0, k], weight[:, i, 0, k:k + 1], None, ALU.mult)
                last.then_inc(s["mix_half"], 1)
                dve.wait_ge(s["mix_half"], b + 1)
                for k in range(K):
                    last = nc.vector.scalar_tensor_tensor(out=mix[:, k], in0=yg[:, 1, k], scalar=weight[:, i, 1, k:k + 1],
                                                          in1=mix[:, k], op0=ALU.mult, op1=ALU.add)
                last.then_inc(s["mix_ready"], 1)

            def mix_stats(b, i, _):
                alone(dve, (s["mix_ready"], b + 1))
                moments(lambda k: mix[:, k, :], st_m, mv_m, K, s["mix_stats"], s["mix_mom"], b + 1)

            def result(b, i, _):
                dve.wait_ge(s["mix_scale"], b + 1)
                for k in range(K):
                    last = nc.vector.tensor_scalar(mix[:, k], mix[:, k], mv_m[:, k, 0:1], rs_m[:, k:k + 1],
                                                   ALU.subtract, ALU.mult)
                last.then_inc(s["results_free"], 1)

            nc.vector.memset(eps[:, 0:1], EPS)
            nc.vector.memset(eps[:, 1:2], EPS * EPS)
            nc.vector.memset(zeros[:], 0.0).then_inc(s["zero_set"], 1)
            nc.vector.memset(ones_b[:], 1.0).then_inc(s["results_free"], 1)
            nc.vector.memset(ones[:], 1.0).then_inc(s["dve_set"], 1)
            dve.wait_ge(s["small"], 16 * 9)
            nc.vector.tensor_copy(bias_parts[:, 0], bias_f[:]).then_inc(s["bias_split"], 1)
            dve.wait_ge(s["bias_split"], 1)
            nc.vector.tensor_tensor(bias_r[:], bias_f[:], bias_parts[:, 0], ALU.subtract).then_inc(s["bias_split"], 1)
            dve.wait_ge(s["bias_split"], 2)
            nc.vector.tensor_copy(bias_parts[:, 1], bias_r[:]).then_inc(s["bias_split"], 1)
            dve.wait_ge(s["bias_split"], 3)
            nc.vector.tensor_tensor(bias_s[:], bias_r[:], bias_parts[:, 1], ALU.subtract).then_inc(s["bias_split"], 1)
            dve.wait_ge(s["bias_split"], 4)
            nc.vector.tensor_copy(bias_parts[:, 2], bias_s[:]).then_inc(s["bias_split"], 1)
            nc.vector.tensor_copy(w_rep[:], w_bc[:].rearrange("d (c n) -> d c n", c=2)[:, :, :, None]
                                  .to_broadcast([D, 2, N, J])).then_inc(s["w_rep_set"], 1)
            dve.wait_ge(s["decay_exp"], 1)
            nc.vector.tensor_scalar(decay[:], decay[:], -1.0, None, ALU.mult).then_inc(s["decay_set"], 1)
            dve.wait_ge(s["pool_set"], 3)
            nc.vector.tensor_copy(spread[:], spread_f[:].rearrange("p a n j -> p a (n j)"))
            nc.vector.tensor_reduce(fold[:], fold_f[:].rearrange("p n j -> p j n"), AX.X, ALU.add)
            nc.vector.tensor_copy(iota_e[:], iota_i[:].rearrange("p (k e) -> p k e", k=K))
            nc.vector.tensor_copy(iota_j[:], iota_ji[:].rearrange("p (j e) -> p j e", e=E))
            nc.vector.tensor_scalar(restart[:], iota_k[:].rearrange("p (e k) -> p e k", e=E), 1.0, None,
                                    ALU.min).then_inc(s["consts"], 1)
            walk(dve, dict(stats=stats, norm=norm, skip=skip_path, dt=dt_gx, rest=rest, drive=drive, scan=scan,
                           weights=weights, y_sum=y_sum, y_norm=y_norm, x1_stats=x1_stats, x1_norm=x1_norm,
                           gate_max=gate_max, softmax=softmax, second=second, starts=starts, slots=slots, tile_turn=tile_turn,
                           mix=mix_results, mix_stats=mix_stats, result=result))

        @block.tensor
        def _(pe):
            def turn_x(b, i, _):
                pe.wait_ge(s["normed"], b + 1)
                after(pe, s["dt_ready"], b)
                after(pe, s["prefix_used"], b - 2)
                for k in range(K):
                    last = nc.tensor.matmul(misc[:, k * P:(k + 1) * P], xn[:, i, k], ident[:], start=True, stop=True,
                                            is_transpose=True)
                last.then_inc(s["turned"], 1)

            def states(b, i, _):
                pe.wait_ge(s["xa_ready"], b + 1)
                nc.tensor.matmul(misc[:], w_rep[:, 0].rearrange("d n j -> d (n j)"), xa[:, i], start=True,
                                 stop=True).then_inc(s["b_ps"], 1)

            def readout(b, i, _):
                pe.wait_ge(s["b_ready"], b + 1)
                nc.tensor.matmul(misc[:], w_rep[:, 1].rearrange("d n j -> d (n j)"), xa[:, i], start=True,
                                 stop=True).then_inc(s["c_ps"], 1)

            def delta(b, i, _):
                pe.wait_ge(s["c_ready"], b + 1)
                nc.tensor.matmul(misc[:], w_dt[:], xa[:, i], start=True, stop=False)
                pe.wait_ge(s["bias_in"], 16)
                nc.tensor.matmul(misc[:], bias[:, BDT_AT:BDT_AT + D], ones_b[:], start=False, stop=True).then_inc(s["z_ps"], 1)

            def rep(b, i, r):
                n = UNITS * b + r
                if r == 0:
                    pe.wait_ge(stacked[i], turns(128, b, i) + 128)
                h, m = divmod(r, J)
                after(pe, s["decayed"], n)
                nc.tensor.matmul(dt_ps[:], spread[:, m], dt_s[:, i, h], start=True, stop=True).then_inc(s["dt_rep"], 1)
                after(pe, s["driven"], n)
                nc.tensor.matmul(gx_ps[:], spread[:, m], gx_s[:, i, h], start=True, stop=True).then_inc(s["gx_rep"], 1)

            def reduce(b, i, r):
                n = UNITS * b + r
                pe.wait_ge(s["weighed"], n + 1)
                if r == 0:
                    after(pe, s["y_ready"], b)
                for k in range(K):
                    last = nc.tensor.matmul(y_ps[:, k * D + r * J:k * D + (r + 1) * J],
                                            ch[:, r % NU, k * P:(k + 1) * P], fold[:], start=True, stop=True)
                last.then_inc(s["reduced"], 1)

            def gate_turn(b, i, _):
                pe.wait_ge(s["x2_ready"], b + 1)
                pe.wait_ge(s["dt_ready"], min(b + 3, SEQS) if isinstance(b, int) else b + 3)
                for k in range(K):
                    last = nc.tensor.matmul(misc[:, k * P:(k + 1) * P], x2[:, i, k], ident[:], start=True, stop=True,
                                            is_transpose=True)
                last.then_inc(s["x2_turned"], 1)

            def gate_logits(b, i, _):
                pe.wait_ge(s["x2_copied"], b + 1)
                for k in range(K):
                    last = nc.tensor.matmul(misc[:, k * E:(k + 1) * E], x2_t[:, k * P:(k + 1) * P], gate[:], start=True,
                                            stop=True)
                last.then_inc(s["logits_ps"], 1)

            def count(b, i, _):
                pe.wait_ge(s["mask_ready"], b + 1)
                m = mask[:].rearrange("p k e -> p (k e)")
                nc.tensor.matmul(misc[:, 0:K * E], before[:], m, start=True, stop=True)
                nc.tensor.matmul(misc[:, K * E:2 * K * E], ones[:], m, start=True, stop=True).then_inc(s["prefix_ready"], 1)

            def tile_turn(b, i, j):
                pe.wait_ge(tile_loaded[j % NX], 16 * (TILES // NX * b + j // NX + 1))
                after(pe, s["tile_lo"], TILES * b + j)
                nc.tensor.matmul(turn[:, 0:P], xt[:, j % NX], ident[:], start=True, stop=True,
                                 is_transpose=True).then_inc(s["tile_turned"], 1)

            picked = {}

            def begin():
                picked.clear()

            def pick(i, j):
                return pe.value_load(expert[0:1, i, j:j + 1], min_val=0, max_val=E - 1)

            def tile_pick(b, i, j):
                if j == 0:
                    alone(pe, (s["routed"], b + 1), (s["w_split_lo"], E), (s["w_ld"], 16))
                picked[i, j] = pick(i, j)

            def tile_up(b, i, j):
                e = picked[i, j] if (i, j) in picked else pick(i, j)
                picked[i, j] = e
                pe.wait_ge(s["tile_lo"], TILES * b + j + 1)
                after(pe, s["tile_relu"], TILES * b + j)
                nc.tensor.matmul(hid_ps[:], ones_b[:, 0:P], bias[:, bass.ds(e * HID, HID)], start=True, stop=False)
                nc.tensor.matmul(hid_ps[:], xt_lo[:, (i + j) % 2], w_hi[:, bass.ds(e * HID, HID)], start=False, stop=False)
                nc.tensor.matmul(hid_ps[:], xt_hi[:, (i + j) % 2], w_lo[:, bass.ds(e * HID, HID)], start=False, stop=False)
                nc.tensor.matmul(hid_ps[:], xt_hi[:, (i + j) % 2], w_hi[:, bass.ds(e * HID, HID)], start=False,
                                 stop=True).then_inc(s["tile_hid"], 1)

            def tile_fold(b, i, j):
                pe.wait_ge(s["tile_relu"], TILES * b + j + 1)
                after(pe, s["fold_copied"], TILES * b + j)
                for c in range(HC):
                    last = nc.tensor.matmul(fold_ps[:, c * P:(c + 1) * P], hid[:, (i + j) % 2, c * P:(c + 1) * P], ident[:],
                                            start=True, stop=True, is_transpose=True)
                last.then_inc(s["tile_folded"], 1)

            def tile_down(b, i, j):
                e = picked[i, j] if (i, j) in picked else pick(i, j)
                pe.wait_ge(s["fold_copied"], TILES * b + j + 1)
                after(pe, s["tile_copied"], TILES * b + j)
                o = out_ps[:, 0:D]
                nc.tensor.matmul(o, ones_b[:, 0:P], bias[:, bass.ds(B2_AT + e * D, D)], start=True, stop=False)
                for c in range(HC):
                    last = nc.tensor.matmul(o, hid_t[:, (i + j) % 2, c * P:(c + 1) * P], w2_f[:, bass.ds(e * HC * D + c * D, D)],
                                            start=False, stop=(c == HC - 1))
                last.then_inc(s["tile_out"], 1)

            pe.wait_ge(s["pool_set"], 3)
            pe.wait_ge(s["w_rep_set"], 1)
            pe.wait_ge(s["consts"], 1)
            walk(pe, dict(begin=begin, tile_pick=tile_pick, turn=turn_x, states=states, readout=readout, delta=delta, rep=rep, reduce=reduce,
                          gate_turn=gate_turn, gate_logits=gate_logits, count=count, tile_turn=tile_turn,
                          tile_up=tile_up, tile_fold=tile_fold, tile_down=tile_down))


def kernel(**inputs):
    import numpy as np
    import concourse.bacc as bacc
    from concourse.bass_utils import run_bass_kernel_spmd

    a = {k: np.asarray(v) for k, v in inputs.items()}
    arrays = {
        "x": a["L0_attn_x"],
        "w_dt_t": a["L0_attn_W_dt"].T,
        "w_bc_t": np.concatenate([a["L0_attn_W_B"], a["L0_attn_W_C"]]).T,
        "biases": np.concatenate([a["L0_ffn_b1"].ravel(), a["L0_ffn_b2"].ravel(), a["L0_attn_b_dt"]]),
        "d_param": a["L0_attn_D_param"],
        "a_log": a["L0_attn_A_log"].reshape(UNITS, J, N).transpose(2, 1, 0).reshape(P, UNITS),
        "gamma": a["L0_attn_gamma"],
        "beta": a["L0_attn_beta"],
        "gate_w": a["L0_ffn_gate_w"],
        "gate_b": a["L0_ffn_gate_b"],
        "w1": a["L0_ffn_w1"],
        "w2": a["L0_ffn_w2"],
    }
    arrays = {k: np.ascontiguousarray(v) for k, v in arrays.items()}
    nc = bacc.Bacc("TRN2", target_bir_lowering=False, num_devices=1)
    args = [nc.dram_tensor(k, v.shape, mybir.dt.from_np(v.dtype), kind="ExternalInput").ap() for k, v in arrays.items()]
    out = nc.dram_tensor("out", (SEQS, T, D), F32, kind="ExternalOutput").ap()
    program(nc, *args, out)
    result = run_bass_kernel_spmd(nc, [arrays], core_ids=[0])
    return result.results[0]["out"]
```

```python
from contextlib import ExitStack

import concourse.bass as bass
from concourse import mybir

F32 = mybir.dt.float32
F32R = mybir.dt.float32r
BF16 = mybir.dt.bfloat16
I32 = mybir.dt.int32
U32 = mybir.dt.uint32
ALU = mybir.AluOpType
ACT = mybir.ActivationFunctionType
AX = mybir.AxisListType

P = 128
EPS = 1e-5
SEQS, T, D, N = 8, 512, 128, 16
E, HID, TOPK = 8, 512, 2
K = T // P
J = P // N
UNITS = D // J
TILES = K * TOPK + E - 1
SLOTS = TILES * P
HC = HID // P
NX = 5
NO = 3
assert TILES % NX == 0 and TILES % NO == 0
TOP_LINKS, SECOND_LINKS, START_LINKS, SLOT_LINKS = 8, 6, 9, 4
NU = 4
FOLD_AT = D - J
NBIAS = E * D + D
BC = NBIAS // P
BDT_AT = E * D


PLAN = (
    ("rep", UNITS, UNITS), ("turn", 4, 1), ("count", 45, 1), ("y_copy", 35, 1), ("y_sum", 36, 1),
    ("scan", UNITS + 1, UNITS), ("weigh", UNITS + 1, UNITS), ("scales", 3, 1), ("tile_keep", 56, TILES),
    ("decay", UNITS, UNITS), ("tile_turn", 52, TILES), ("drive", UNITS, UNITS), ("tile_load", 50, TILES),
    ("y_scale", 37, 1), ("x1_scale", 39, 1), ("channels", 4, 1), ("tile_up", 53, TILES), ("states_copy", 7, 1),
    ("readout_copy", 8, 1), ("gate_copy", 41, 1), ("tile_fold", 54, TILES), ("tile_copy", 54, TILES),
    ("tile_named", 53, TILES), ("load", 0, 1), ("fill", UNITS, 1), ("weights_2", 28, 1), ("clear", 36, 2),
    ("weights", UNITS + 4, E), ("stats", 2, 1), ("norm", 3, 1), ("softplus", 5, 1), ("dt", 6, 1),
    ("split", 6, 1), ("rest", 8, 1), ("stack", 9, 1), ("reload", 33, 1), ("skip", 10, 1), ("y_norm", 37, 1),
    ("x1_norm", 39, 1), ("gate_max", 41, 1), ("x1_stats", 38, 1), ("gate_exp", 42, 1), ("softmax", 42, 1),
    ("second", 43, 1), ("slots", 46, 1), ("mix", 76, 1), ("mix_stats", 77, 1), ("mix_scale", 78, 1),
    ("result", 79, 1), ("reduce", UNITS + 3, UNITS), ("y_turn", 35, 1), ("starts", 45, 1),
    ("tile_down", 55, TILES), ("delta", 4, 1), ("states", 7, 1), ("readout", 7, 1), ("gate_turn", 40, 1),
    ("tile_pick", 52, TILES), ("scatter", 46, 4), ("gather", 70, 4), ("gate_logits", 41, 1),
)
ONCE = ("fill", "weights", "weights_2", "clear")
LAST_LAG = max(at + times - 1 for _, at, times in PLAN) // UNITS


def order():
    return [(kind, half - (at + r) // UNITS, r) for half in (0, 1) for u in range(UNITS)
            for kind, at, times in PLAN for r in range(times) if (at + r) % UNITS == u]


def program(nc, x, w_dt_t, w_bc_t, biases, b1, d_param, a_log, gamma, beta, gate_w, gate_b, w1, w2, out):
    slots_in = [nc.dram_tensor(f"slots_in{i}", [SLOTS, D], F32, kind="Internal").ap() for i in range(2)]
    slots_out = [nc.dram_tensor(f"slots_out{i}", [SLOTS, D], F32, kind="Internal").ap() for i in range(2)]
    bias_rows = nc.dram_tensor("bias_rows", [3, NBIAS], BF16, kind="Internal").ap()
    x_in = x.rearrange("b (k p) d -> b p k d", p=P)
    x_out = out.rearrange("b (k p) d -> b p k d", p=P)

    with ExitStack() as ctx:
        def sb(name, shape, dt=F32):
            return ctx.enter_context(nc.sbuf_tensor(name, shape, dt))

        def bank(name):
            return ctx.enter_context(nc.psum_tensor(name, [P, 512], F32))

        ident = sb("ident", [P, P])
        ones = sb("ones", [P, P])
        before = sb("before", [P, P])
        spread_f = sb("spread_f", [P, J, N, J])
        spread = sb("spread", [P, J, P], F32R)
        fold_f = sb("fold_f", [P, N, J])
        fold = sb("fold", [P, FOLD_AT + D])
        ones_b = sb("ones_b", [3, 512], BF16)
        iota_i = sb("iota_i", [P, K * E], I32)
        iota_k = sb("iota_k", [P, E * K], I32)
        iota_e = sb("iota_e", [P, K, E])
        restart = sb("restart", [P, E, K])
        iota_ji = sb("iota_ji", [1, TILES * E], I32)
        iota_j = sb("iota_j", [1, TILES, E])
        eps = sb("eps", [P, 2])
        w_dt = sb("w_dt", [D, D])
        w_bc = sb("w_bc", [D, 2 * N])
        w_rep = sb("w_rep", [D, 2, N, J])
        decay = sb("decay", [P, UNITS])
        gam = sb("gam", [D, 1])
        bet = sb("bet", [D, 1])
        skip = sb("skip", [P, D])
        b1_t = sb("b1_t", [P, E * HC])
        gate = sb("gate", [D, E])
        gate_bias = sb("gate_bias", [P, E])
        bias_f = sb("bias_f", [P, BC])
        bias_r = sb("bias_r", [P, BC])
        bias_s = sb("bias_s", [P, BC])
        bias_parts = sb("bias_parts", [P, 3, BC], BF16)
        bias = sb("bias", [3, NBIAS], BF16)
        w1_f = sb("w1_f", [P, 2, HID])
        w2_f = sb("w2_f", [P, E * HC * D])
        w_hi = sb("w_hi", [P, E * HID], F32R)
        w_lo = sb("w_lo", [P, E * HID], F32R)
        zeros = sb("zeros", [P, D])

        xs = sb("xs", [P, 2, K, D])
        xr = sb("xr", [P, K, D])
        st = sb("st", [P, K, 6])
        mv = sb("mv", [P, 2, K, 2])
        lv = sb("lv", [P, 2, K])
        rs = sb("rs", [P, 2, 2, K])
        u_t = sb("u_t", [P, 2, K, D])
        xn = sb("xn", [P, 2, K, D])
        xa = sb("xa", [D, 2, T])
        sp_l = sb("sp_l", [D, T])
        dt = sb("dt", [D, T])
        gx = sb("gx", [D, T])
        dt_hi = sb("dt_hi", [D, T], F32R)
        dt_lo = sb("dt_lo", [D, T], F32R)
        gx_hi = sb("gx_hi", [D, T], F32R)
        gx_lo = sb("gx_lo", [D, T], F32R)
        dt_s = sb("dt_s", [P, 2, 2, T], F32R)
        gx_s = sb("gx_s", [P, 2, 2, T], F32R)
        b_rep = sb("b_rep", [P, 2, T])
        c_rep = sb("c_rep", [P, 2, T])
        ab = sb("ab", [P, 2, T])
        bx = sb("bx", [P, 2, T])
        hs = sb("hs", [P, NU, T])
        ch = sb("ch", [P, NU, T])
        y = sb("y", [P, K, D])
        st_y = sb("st_y", [P, K, 6])
        mv_y = sb("mv_y", [P, K, 2])
        lv_y = sb("lv_y", [P, K])
        rs_y = sb("rs_y", [P, K])
        st_1 = sb("st_1", [P, K, 6])
        mv_1 = sb("mv_1", [P, K, 2])
        lv_1 = sb("lv_1", [P, K])
        rs_1 = sb("rs_1", [P, K])
        x1 = sb("x1", [P, SEQS * K, D])
        x2 = sb("x2", [P, 2, K, D])
        yx_t = sb("yx_t", [D, T])
        logit = sb("logit", [P, K, E])
        r_max = sb("r_max", [P, K])
        r_sub = sb("r_sub", [P, K, E])
        r_exp = sb("r_exp", [P, K, E])
        r_sum = sb("r_sum", [P, K])
        prob = sb("prob", [P, K, E])
        eq = sb("eq", [P, K, E])
        cand = sb("cand", [P, K, E])
        pick = sb("pick", [P, K])
        best = sb("best", [P, TOPK, K])
        hot = sb("hot", [P, TOPK, K, E])
        prob_2 = sb("prob_2", [P, K, E])
        mask = sb("mask", [P, K, E])
        tot = sb("tot", [P, E, K])
        run = sb("run", [P, E, K])
        cnt_i = sb("cnt_i", [P, E], I32)
        til_i = sb("til_i", [P, E], I32)
        til = sb("til", [P, E])
        end = sb("end", [P, E])
        beg = sb("beg", [P, E])
        pos_a = sb("pos_a", [P, E, K])
        pos_b = sb("pos_b", [P, E, K])
        pos_e = sb("pos_e", [P, K, E])
        pos_h = sb("pos_h", [P, TOPK * K, E])
        pos_f = sb("pos_f", [P, TOPK * K])
        pos = sb("pos", [P, 2, TOPK * K], U32)
        weight = sb("weight", [P, 2, TOPK, K])
        past = sb("past", [1, TILES, E])
        exp_f = sb("exp_f", [1, TILES])
        expert = sb("expert", [1, 2, TILES], I32)
        xt = sb("xt", [P, NX, D])
        xt_hi = sb("xt_hi", [D, 2, P], F32R)
        xt_lo = sb("xt_lo", [D, 2, P], F32R)
        hid = sb("hid", [P, 2, HID])
        hid_t = sb("hid_t", [P, 2, HID])
        ot = sb("ot", [P, NO, D])
        yg = sb("yg", [P, TOPK, K, D])
        mix = sb("mix", [P, K, D])
        st_m = sb("st_m", [P, K, 6])
        mv_m = sb("mv_m", [P, K, 2])
        lv_m = sb("lv_m", [P, K])
        rs_m = sb("rs_m", [P, K])

        dt_ps = bank("dt_ps")
        gx_ps = bank("gx_ps")
        y_ps = bank("y_ps")
        misc = bank("misc")
        turn = bank("turn")
        out_ps = bank("out_ps")
        hid_ps = bank("hid_ps")
        fold_ps = bank("fold_ps")

        names = """consts results_free pool_set mix_half prefix_used dve_set small bias_split bias_out bias_in w_ld
            w_split_hi w_split_lo w_rep_set decay_exp decay_set zero_set zeroed stats moments logs scales normed
            turned xa_ready b_ps b_ready c_ps c_ready z_ps sp_abs sp_exp sp_log dt_ready gx_ready dt_hi_ready
            gx_hi_ready dt_lo_ready gx_lo_ready dt_rep gx_rep decayed driven scanned weighed reduced skip_ready
            y_ready y_stats y_mom y_copied y_turned y_log y_scale y_normed x1_ready x1_stats x1_mom x1_log x1_scale
            x2_ready x_reloaded x2_turned x2_copied logits_ps logits_ready max_ready top_chain second_chain
            start_chain slot_chain route_max route_exp mask_ready prefix_ready routed tile_turned tile_hi tile_lo
            tile_hid hid_ready tile_folded hid_t_ready tile_out tile_copied mix_ready mix_stats mix_mom mix_log
            mix_scale out_ready written""".split()
        s = {n: ctx.enter_context(nc.semaphore(n)) for n in names}
        x_loaded = [ctx.enter_context(nc.semaphore(f"x_loaded{i}")) for i in range(2)]
        tile_loaded = [ctx.enter_context(nc.semaphore(f"tile_loaded{i}")) for i in range(NX)]
        stacked = [ctx.enter_context(nc.semaphore(f"stacked{i}")) for i in range(2)]
        scattered = [ctx.enter_context(nc.semaphore(f"scattered{i}")) for i in range(2)]
        gathered = [ctx.enter_context(nc.semaphore(f"gathered{i}")) for i in range(2)]
        w1_loaded = [ctx.enter_context(nc.semaphore(f"w1_loaded{i}")) for i in range(2)]
        stored = [ctx.enter_context(nc.semaphore(f"stored{i}")) for i in range(NO)]
        steps = order()

        def after(eng, sem, n):
            if not (isinstance(n, int) and n <= 0):
                eng.wait_ge(sem, n)

        def alone(eng, *waits):
            for _, n in waits:
                if not isinstance(n, int):
                    eng.compute_val(n)
            eng.wait_ge(s["dve_set"], 1)
            for sem, n in waits:
                after(eng, sem, n)

        def chain(eng, sem, per, index):
            n = [0]

            def link(ins):
                n[0] += 1
                ins.then_inc(sem, 1)
                eng.wait_ge(sem, per * index + n[0])
            return link

        def turns(per, b, i):
            return per // 2 * (b - i)

        def tile_seen(b, j, n):
            return TILES * b + (j - n + 1 if j >= n else 0)

        def walk(eng, parts, begun=()):
            def iteration(it, first, last):
                if "begin" in parts:
                    parts["begin"]()
                for kind, c, r in steps:
                    if kind in parts and 2 * first + c >= 0 and 2 * last + c < SEQS and (
                            kind not in ONCE or 2 * last + c == 0) and not (kind in begun and c == last == 0):
                        parts[kind](2 * it + c, c % 2, r)

            ahead = LAST_LAG // 2
            for it in range(ahead):
                iteration(it, it, it)
            with eng.Fori(ahead, SEQS // 2) as it:
                iteration(it, ahead, SEQS // 2 - 1)
            for it in range(SEQS // 2, SEQS // 2 + ahead):
                iteration(it, it, it)

        block = ctx.enter_context(nc.Block())

        @block.sync
        def _(sp):
            def load(b, i, _):
                if isinstance(b, int) and b < 2:
                    return
                alone(sp, (s["skip_ready"], 2 * b - 3))
                sp.dma_start(xs[:, i], x_in[b]).then_inc(x_loaded[i], 16)

            def reload(b, i, _):
                alone(sp, (s["x1_ready"], b))
                sp.dma_start(xr[:], x_in[b]).then_inc(s["x_reloaded"], 16)

            def weights(b, i, c):
                if c + 2 < E:
                    sp.wait_ge(s["w_split_lo"], c + 1)
                    sp.dma_start(w1_f[:, c % 2], w1[c + 2]).then_inc(w1_loaded[c % 2], 16)

            def fill(b, i, _):
                for e in range(2):
                    sp.dma_start(w1_f[:, e], w1[e]).then_inc(w1_loaded[e], 16)

            def weights_2(b, i, _):
                sp.dma_start(w2_f[:].rearrange("p (e c d) -> p e c d", e=E, c=HC),
                             w2.rearrange("e (c p) d -> p e c d", p=P)).then_inc(s["w_ld"], 16)
                sp.wait_ge(s["zero_set"], 1)
                sp.dma_start(mix[:, 0, 0:E], zeros[:, 0:E]).then_inc(s["written"], 16)

            def clear(b, i, r):
                sp.dma_start(slots_in[r].rearrange("(j p) d -> p j d", p=P),
                             zeros[:, None, :].to_broadcast([P, TILES, D])).then_inc(s["zeroed"], 16)

            def stack(b, i, _):
                if not isinstance(b, int):
                    sp.compute_val(b + 1)
                alone(sp, (s["dt_rep"], UNITS * (b - 1)), (s["gx_rep"], UNITS * (b - 1)))
                for hi, lo, hi_sem, lo_sem, dst in ((dt_hi, dt_lo, s["dt_hi_ready"], s["dt_lo_ready"], dt_s),
                                                    (gx_hi, gx_lo, s["gx_hi_ready"], s["gx_lo_ready"], gx_s)):
                    alone(sp, (hi_sem, b + 1))
                    for h in range(2):
                        sp.dma_start(dst[0:64, i, h].bitcast(F32),
                                     hi[64 * h:64 * h + 64, :].bitcast(F32)).then_inc(stacked[i], 16)
                    alone(sp, (lo_sem, b + 1))
                    for h in range(2):
                        sp.dma_start(dst[64:128, i, h].bitcast(F32),
                                     lo[64 * h:64 * h + 64, :].bitcast(F32)).then_inc(stacked[i], 16)

            def tile_load(b, i, j):
                if j == 0:
                    alone(sp, (scattered[i], turns(16 * TOPK * K, b, i) + 16 * TOPK * K), (s["tile_turned"], TILES * b))
                else:
                    after(sp, s["tile_turned"], tile_seen(b, j, NX))
                sp.dma_start(xt[:, j % NX], slots_in[i][j * P:(j + 1) * P, :]).then_inc(tile_loaded[j % NX], 16)

            def tile_keep(b, i, j):
                if j == 0:
                    alone(sp, (s["results_free"], b), (s["tile_copied"], TILES * b + j + 1))
                else:
                    sp.wait_ge(s["tile_copied"], TILES * b + j + 1)
                sp.dma_start(slots_out[i][j * P:(j + 1) * P, :], ot[:, j % NO]).then_inc(stored[j % NO], 16)

            def result(b, i, _):
                alone(sp, (s["out_ready"], b + 1))
                sp.dma_start(x_out[b], mix[:]).then_inc(s["written"], 16)

            sp.dma_start(xs[:, 0], x_in[0]).then_inc(x_loaded[0], 16)
            for dst, src in ((bias_f[:], biases.rearrange("(p c) -> p c", p=P)), (w_dt[:], w_dt_t), (w_bc[:], w_bc_t),
                             (decay[:], a_log), (gam[:], gamma[:, None]), (bet[:], beta[:, None]),
                             (skip[:], d_param[None, :].to_broadcast([P, D])), (gate[:], gate_w), (b1_t[:], b1),
                             (gate_bias[:], gate_b[None, :].to_broadcast([P, E]))):
                sp.dma_start(dst, src).then_inc(s["small"], 16)
            sp.dma_start(xs[:, 1], x_in[1]).then_inc(x_loaded[1], 16)
            sp.wait_ge(s["bias_split"], 5)
            for r in range(3):
                sp.dma_start(bias_rows[r].rearrange("(p c) -> p c", p=P), bias_parts[:, r]).then_inc(s["bias_out"], 16)
            sp.wait_ge(s["bias_out"], 48)
            sp.dma_start(bias[:], bias_rows).then_inc(s["bias_in"], 16)
            walk(sp, dict(load=load, fill=fill, weights_2=weights_2, clear=clear, reload=reload,
                          weights=weights, stack=stack, tile_load=tile_load,
                          tile_keep=tile_keep, result=result))
            sp.wait_ge(s["written"], 16 * (SEQS + 1))

        @block.gpsimd
        def _(pool):
            def weigh(b, i, r):
                n = UNITS * b + r
                pool.wait_ge(s["scanned"], n + 1)
                if r == 0:
                    pool.wait_ge(s["c_ready"], b + 1)
                after(pool, s["reduced"], n - NU + 1)
                nc.gpsimd.tensor_tensor(ch[:, r % NU], hs[:, r % NU], c_rep[:, i], ALU.mult).then_inc(s["weighed"], 1)

            def scatter(b, i, r):
                if r == 0:
                    alone(pool, (s["routed"], b + 1), (s["zeroed"], 16 * 2),
                          *((loaded, 16 * TILES // NX * (b - 1)) for loaded in tile_loaded))
                for q in (2 * r, 2 * r + 1):
                    nc.gpsimd.indirect_dma_start(
                        out=slots_in[i], out_offset=bass.IndirectOffsetOnAxis(pos[:, i, q:q + 1], 0),
                        in_=x2[:, i, q % K, :], in_offset=None).then_inc(scattered[i], 16)

            def gather(b, i, r):
                if r == 0:
                    alone(pool, (s["results_free"], b + 1), *((done, 16 * TILES // NO * (b + 1)) for done in stored))
                for q in (2 * r, 2 * r + 1):
                    nc.gpsimd.indirect_dma_start(
                        out=yg[:, q // K, q % K, :], out_offset=None, in_=slots_out[i],
                        in_offset=bass.IndirectOffsetOnAxis(pos[:, i, q:q + 1], 0)).then_inc(gathered[i], 16)

            def skip_path(b, i, _):
                pool.wait_ge(s["skip_ready"], 2 * b + 1)
                nc.gpsimd.tensor_tensor(u_t[:, i], u_t[:, i], skip[:, None, :].to_broadcast([P, K, D]),
                                        ALU.mult).then_inc(s["skip_ready"], 1)

            def dt_gx(b, i, _):
                pool.wait_ge(s["dt_ready"], b + 1)
                nc.gpsimd.tensor_tensor(gx[:], dt[:], xa[:, i], ALU.mult).then_inc(s["gx_ready"], 1)

            def result(b, i, _):
                pool.wait_ge(s["results_free"], b + 2)
                nc.gpsimd.tensor_tensor(mix[:], mix[:], x1[:, bass.ds(K * b, K), :], ALU.add).then_inc(s["out_ready"], 1)

            nc.gpsimd.memset(ident[:], 0.0)
            nc.gpsimd.memset(spread_f[:], 0.0)
            nc.gpsimd.memset(fold_f[:], 0.0)
            nc.gpsimd.memset(before[:], 1.0)
            nc.gpsimd.memset(fold[:], 0.0)
            nc.gpsimd.iota(iota_i[:], pattern=[[0, K], [1, E]], base=0, channel_multiplier=0)
            nc.gpsimd.iota(iota_k[:], pattern=[[0, E], [1, K]], base=0, channel_multiplier=0)
            nc.gpsimd.iota(iota_ji[:], pattern=[[1, TILES], [0, E]], base=0, channel_multiplier=0).then_inc(s["pool_set"], 1)
            pool.wait_ge(s["pool_set"], 1)
            nc.gpsimd.affine_select(out=ident[:], in_=ident[:], compare_op=ALU.not_equal, fill=1.0, base=0,
                                    pattern=[[-1, P]], channel_multiplier=1)
            nc.gpsimd.affine_select(out=before[:], in_=before[:], compare_op=ALU.is_gt, fill=0.0, base=0,
                                    pattern=[[1, P]], channel_multiplier=-1)
            nc.gpsimd.affine_select(out=fold_f[:], in_=fold_f[:], compare_op=ALU.not_equal, fill=1.0, base=0,
                                    pattern=[[-J, N], [-1, J]], channel_multiplier=1)
            nc.gpsimd.affine_select(out=spread_f[:], in_=spread_f[:], compare_op=ALU.not_equal, fill=1.0, base=0,
                                    pattern=[[-J, J], [0, N], [-1, J]], channel_multiplier=1).then_inc(s["pool_set"], 1)
            pool.wait_ge(s["pool_set"], 2)
            nc.gpsimd.affine_select(out=spread_f[:], in_=spread_f[:], compare_op=ALU.not_equal, fill=1.0, base=-64,
                                    pattern=[[-J, J], [0, N], [-1, J]], channel_multiplier=1).then_inc(s["pool_set"], 1)
            walk(pool, dict(weigh=weigh, skip=skip_path, dt=dt_gx, scatter=scatter, gather=gather, result=result))

        @block.scalar
        def _(act):
            def rsqrt(src, logs, dst, log_sem, done, n):
                nc.scalar.activation(logs, src, ACT.Ln, bias=eps[:, 0:1]).then_inc(log_sem, 1)
                act.wait_ge(log_sem, n)
                nc.scalar.activation(dst, logs, ACT.Exp, scale=-0.5).then_inc(done, 1)

            def scales(b, i, _):
                act.wait_ge(s["moments"], b + 1)
                nc.scalar.activation(lv[:, 0], mv[:, i, :, 1], ACT.Ln, bias=eps[:, 0:1])
                nc.scalar.activation(lv[:, 1], mv[:, i, :, 1], ACT.Ln, bias=eps[:, 1:2],
                                     scale=1.0 + EPS).then_inc(s["logs"], 1)
                act.wait_ge(s["logs"], b + 1)
                nc.scalar.activation(rs[:, i], lv[:], ACT.Exp, scale=-0.5).then_inc(s["scales"], 1)

            def channels(b, i, _):
                act.wait_ge(s["turned"], b + 1)
                nc.scalar.activation(xa[:, i], misc[:], ACT.Identity, bias=bet[:, 0:1],
                                     scale=gam[:, 0:1]).then_inc(s["xa_ready"], 1)

            def states_copy(b, i, _):
                act.wait_ge(s["b_ps"], b + 1)
                nc.scalar.activation(b_rep[:, i], misc[:], ACT.Copy).then_inc(s["b_ready"], 1)

            def readout_copy(b, i, _):
                act.wait_ge(s["c_ps"], b + 1)
                nc.scalar.activation(c_rep[:, i], misc[:], ACT.Copy).then_inc(s["c_ready"], 1)

            def softplus(b, i, _):
                act.wait_ge(s["z_ps"], b + 1)
                nc.scalar.activation(sp_l[:], misc[:], ACT.Abs).then_inc(s["sp_abs"], 1)
                act.wait_ge(s["sp_abs"], b + 1)
                nc.scalar.activation(sp_l[:], sp_l[:], ACT.Exp, scale=-1.0).then_inc(s["sp_exp"], 1)
                act.wait_ge(s["sp_exp"], b + 1)
                nc.scalar.activation(sp_l[:], sp_l[:], ACT.Ln, bias=ones[:, 0:1]).then_inc(s["sp_log"], 1)

            def split(b, i, _):
                act.wait_ge(s["dt_ready"], b + 1)
                after(act, stacked[1 - i], 64 * (b - 1 + i) if i == 0 else 64 * (b + 1))
                nc.scalar.activation(dt_hi[:], dt[:], ACT.Copy).then_inc(s["dt_hi_ready"], 1)
                act.wait_ge(s["gx_ready"], b + 1)
                nc.scalar.activation(gx_hi[:], gx[:], ACT.Copy).then_inc(s["gx_hi_ready"], 1)

            def decay_(b, i, r):
                n = UNITS * b + r
                act.wait_ge(s["dt_rep"], n + 1)
                after(act, s["scanned"], n - 1)
                nc.scalar.activation(ab[:, r % 2], dt_ps[:], ACT.Exp, scale=decay[:, r:r + 1]).then_inc(s["decayed"], 1)

            def weights(b, i, c):
                act.wait_ge(w1_loaded[c % 2], 16 * (c // 2 + 1))
                nc.scalar.activation(w_hi[:, c * HID:(c + 1) * HID], w1_f[:, c % 2],
                                     ACT.Copy).then_inc(s["w_split_hi"], 1)

            def y_copy(b, i, _):
                act.wait_ge(s["reduced"], UNITS * (b + 1))
                after(act, s["logits_ps"], b)
                nc.scalar.activation(yx_t[:], y_ps[:], ACT.Copy).then_inc(s["y_copied"], 1)

            def y_scale(b, i, _):
                act.wait_ge(s["y_mom"], b + 1)
                rsqrt(mv_y[:, :, 1], lv_y[:], rs_y[:], s["y_log"], s["y_scale"], b + 1)

            def x1_scale(b, i, _):
                act.wait_ge(s["x1_mom"], b + 1)
                rsqrt(mv_1[:, :, 1], lv_1[:], rs_1[:], s["x1_log"], s["x1_scale"], b + 1)

            def gate_copy(b, i, _):
                act.wait_ge(s["x2_turned"], b + 1)
                nc.scalar.activation(yx_t[:], misc[:], ACT.Copy).then_inc(s["x2_copied"], 1)

            def gate_exp(b, i, _):
                act.wait_ge(s["route_max"], b + 1)
                nc.scalar.activation(r_exp[:], r_sub[:], ACT.Exp).then_inc(s["route_exp"], 1)

            def tile_turn(b, i, j):
                act.wait_ge(s["tile_turned"], TILES * b + j + 1)
                after(act, s["tile_hid"], TILES * b + j - 1)
                nc.scalar.activation(xt_hi[:, (i + j) % 2], turn[:, 0:P], ACT.Copy).then_inc(s["tile_hi"], 1)

            def tile_up(b, i, j):
                act.wait_ge(s["tile_hid"], TILES * b + j + 1)
                after(act, s["tile_folded"], TILES * b + j - 1)
                nc.scalar.activation(hid[:, (i + j) % 2], hid_ps[:], ACT.Copy).then_inc(s["hid_ready"], 1)

            picked = {}

            def begin():
                picked.clear()

            def pick(i, j):
                return act.value_load(expert[0:1, i, j:j + 1], min_val=0, max_val=E - 1)

            def tile_named(b, i, j):
                if j == 0:
                    alone(act, (s["routed"], b + 1))
                picked[i, j] = pick(i, j)

            def tile_copy(b, i, j):
                e = picked[i, j] if (i, j) in picked else pick(i, j)
                act.wait_ge(s["tile_folded"], TILES * b + j + 1)
                after(act, s["tile_out"], TILES * b + j - 1)
                for c in range(HC):
                    last = nc.scalar.activation(hid_t[:, (i + j) % 2, c * P:(c + 1) * P], fold_ps[:, c * P:(c + 1) * P],
                                                ACT.Relu, bias=b1_t[:, bass.ds(e * HC + c, 1)])
                last.then_inc(s["hid_t_ready"], 1)

            def tile_keep(b, i, j):
                act.wait_ge(s["tile_out"], TILES * b + j + 1)
                after(act, stored[j % NO], 16 * (TILES // NO * b + j // NO))
                nc.scalar.activation(ot[:, j % NO], out_ps[:, 0:D], ACT.Copy).then_inc(s["tile_copied"], 1)

            def mix_scale(b, i, _):
                act.wait_ge(s["mix_mom"], b + 1)
                rsqrt(mv_m[:, :, 1], lv_m[:], rs_m[:], s["mix_log"], s["mix_scale"], b + 1)

            act.preload_act_table_set("natural_log_exp_and_others")
            act.wait_ge(s["dve_set"], 1)
            scales(0, 0, 0)
            act.wait_ge(s["small"], 16 * 10)
            nc.scalar.activation(decay[:], decay[:], ACT.Exp).then_inc(s["decay_exp"], 1)
            act.wait_ge(s["decay_set"], 1)
            walk(act, dict(begin=begin, tile_named=tile_named, scales=scales, channels=channels,
                           states_copy=states_copy, readout_copy=readout_copy,
                           softplus=softplus, split=split, decay=decay_, weights=weights, y_copy=y_copy, y_scale=y_scale,
                           x1_scale=x1_scale, gate_copy=gate_copy, gate_exp=gate_exp, tile_turn=tile_turn,
                           tile_up=tile_up, tile_copy=tile_copy, tile_keep=tile_keep, mix_scale=mix_scale),
                 begun=("scales",))

        @block.vector
        def _(dve):
            def moments(src, st_, mv_, n_tiles, st_sem, mv_sem, n):
                for k in range(n_tiles):
                    last = nc.vector.bn_stats(out=st_[:, k, :], in_=src(k))
                last.then_inc(st_sem, 1)
                alone(dve, (st_sem, n))
                for k in range(n_tiles):
                    last = nc.vector.bn_aggr(out=mv_[:, k, :], in_=st_[:, k, :])
                last.then_inc(mv_sem, 1)

            def stats(b, i, _):
                alone(dve, (x_loaded[i], turns(16, b, i) + 16))
                moments(lambda k: xs[:, i, k, :], st, mv[:, i], K, s["stats"], s["moments"], b + 1)

            def norm(b, i, _):
                dve.wait_ge(s["scales"], b + 1)
                after(dve, s["turned"], b - 1)
                for k in range(K):
                    last = nc.vector.tensor_scalar(xn[:, i, k], xs[:, i, k], mv[:, i, k, 0:1], rs[:, i, 1, k:k + 1],
                                                   ALU.subtract, ALU.mult)
                last.then_inc(s["normed"], 1)

            def skip_path(b, i, _):
                for k in range(K):
                    last = nc.vector.tensor_scalar(u_t[:, i, k], xs[:, i, k], mv[:, i, k, 0:1], rs[:, i, 0, k:k + 1],
                                                   ALU.subtract, ALU.mult)
                last.then_inc(s["skip_ready"], 1)

            def dt_gx(b, i, _):
                dve.wait_ge(s["sp_log"], b + 1)
                nc.vector.scalar_tensor_tensor(out=dt[:], in0=misc[:], scalar=0.0, in1=sp_l[:], op0=ALU.max,
                                               op1=ALU.add).then_inc(s["dt_ready"], 1)

            def rest(b, i, _):
                dve.wait_ge(s["dt_hi_ready"], b + 1)
                nc.vector.tensor_tensor(dt_lo[:], dt[:], dt_hi[:].bitcast(F32), ALU.subtract).then_inc(s["dt_lo_ready"], 1)
                dve.wait_ge(s["gx_hi_ready"], b + 1)
                nc.vector.tensor_tensor(gx_lo[:], gx[:], gx_hi[:].bitcast(F32), ALU.subtract).then_inc(s["gx_lo_ready"], 1)

            def drive(b, i, r):
                n = UNITS * b + r
                if r == 0:
                    dve.wait_ge(s["b_ready"], b + 1)
                dve.wait_ge(s["gx_rep"], n + 1)
                after(dve, s["scanned"], n - 1)
                nc.vector.tensor_tensor(bx[:, r % 2], gx_ps[:], b_rep[:, i], ALU.mult).then_inc(s["driven"], 1)

            def scan(b, i, r):
                n = UNITS * b + r
                dve.wait_ge(s["decayed"], n + 1)
                dve.wait_ge(s["driven"], n + 1)
                after(dve, s["weighed"], n - NU + 1)
                nc.vector.tensor_tensor_scan(hs[:, r % NU], ab[:, r % 2], bx[:, r % 2], 0.0, ALU.mult,
                                             ALU.add).then_inc(s["scanned"], 1)

            def weights(b, i, c):
                cols = slice(c * HID, (c + 1) * HID)
                dve.wait_ge(s["w_split_hi"], c + 1)
                nc.vector.tensor_tensor(w_lo[:, cols], w1_f[:, c % 2], w_hi[:, cols].bitcast(F32),
                                        ALU.subtract).then_inc(s["w_split_lo"], 1)

            def y_sum(b, i, _):
                dve.wait_ge(s["y_turned"], b + 1)
                dve.wait_ge(s["skip_ready"], 2 * b + 2)
                nc.vector.tensor_tensor(y[:], turn[:].rearrange("p (k d) -> p k d", k=K), u_t[:, i],
                                        ALU.add).then_inc(s["y_ready"], 1)
                alone(dve, (s["y_ready"], b + 1))
                moments(lambda k: y[:, k, :], st_y, mv_y, K, s["y_stats"], s["y_mom"], b + 1)

            def y_norm(b, i, _):
                dve.wait_ge(s["y_scale"], b + 1)
                for k in range(K):
                    last = nc.vector.tensor_scalar(y[:, k], y[:, k], mv_y[:, k, 0:1], rs_y[:, k:k + 1],
                                                   ALU.subtract, ALU.mult)
                last.then_inc(s["y_normed"], 1)
                dve.wait_ge(s["y_normed"], b + 1)
                dve.wait_ge(s["x_reloaded"], 16 * (b + 1))
                nc.vector.tensor_tensor(x1[:, bass.ds(K * b, K), :], y[:], xr[:], ALU.add).then_inc(s["x1_ready"], 1)

            def x1_stats(b, i, _):
                alone(dve, (s["x1_ready"], b + 1))
                moments(lambda k: x1[:, bass.ds(K * b + k, 1), :], st_1, mv_1, K, s["x1_stats"], s["x1_mom"], b + 1)

            def x1_norm(b, i, _):
                dve.wait_ge(s["x1_scale"], b + 1)
                after(dve, scattered[i], turns(16 * TOPK * K, b, i))
                after(dve, s["x2_turned"], b - 1)
                for k in range(K):
                    last = nc.vector.tensor_scalar(x2[:, i, k], x1[:, bass.ds(K * b + k, 1), :], mv_1[:, k, 0:1],
                                                   rs_1[:, k:k + 1], ALU.subtract, ALU.mult)
                last.then_inc(s["x2_ready"], 1)

            def by_tile(a):
                return a[:, :, None].to_broadcast([P, K, E])

            def gate_max(b, i, _):
                dve.wait_ge(s["logits_ps"], b + 1)
                nc.vector.tensor_tensor(logit[:], misc[:, 0:K * E].rearrange("p (k e) -> p k e", k=K),
                                        gate_bias[:, None, :].to_broadcast([P, K, E]), ALU.add).then_inc(s["logits_ready"], 1)
                dve.wait_ge(s["logits_ready"], b + 1)
                nc.vector.tensor_reduce(r_max[:], logit[:], AX.X, ALU.max).then_inc(s["max_ready"], 1)
                dve.wait_ge(s["max_ready"], b + 1)
                nc.vector.tensor_tensor(r_sub[:], logit[:], by_tile(r_max), ALU.subtract).then_inc(s["route_max"], 1)

            def top(link, c, p):
                link(nc.vector.tensor_reduce(best[:, c], p[:], AX.X, ALU.max))
                link(nc.vector.tensor_tensor(eq[:], p[:], by_tile(best[:, c]), ALU.is_equal))
                link(nc.vector.scalar_tensor_tensor(out=cand[:], in0=eq[:], scalar=-float(E), in1=iota_e[:],
                                                    op0=ALU.mult, op1=ALU.add))
                link(nc.vector.tensor_reduce(pick[:], cand[:], AX.X, ALU.min))

            def softmax(b, i, _):
                link = chain(dve, s["top_chain"], TOP_LINKS, b)
                dve.wait_ge(s["route_exp"], b + 1)
                link(nc.vector.tensor_reduce(r_sum[:], r_exp[:], AX.X, ALU.add))
                link(nc.vector.reciprocal(r_sum[:], r_sum[:]))
                link(nc.vector.tensor_tensor(prob[:], r_exp[:], by_tile(r_sum), ALU.mult))
                top(link, 0, prob)
                link(nc.vector.tensor_tensor(hot[:, 0], cand[:], by_tile(pick), ALU.is_equal))

            def second(b, i, _):
                link = chain(dve, s["second_chain"], SECOND_LINKS, b)
                link(nc.vector.scalar_tensor_tensor(out=prob_2[:], in0=hot[:, 0], scalar=-2.0, in1=prob[:],
                                                    op0=ALU.mult, op1=ALU.add))
                top(link, 1, prob_2)
                link(nc.vector.tensor_tensor(hot[:, 1], cand[:], by_tile(pick), ALU.is_equal))
                nc.vector.tensor_tensor(mask[:], hot[:, 0], hot[:, 1], ALU.add).then_inc(s["mask_ready"], 1)

            def starts(b, i, _):
                link = chain(dve, s["start_chain"], START_LINKS, b)
                dve.wait_ge(s["prefix_ready"], b + 1)
                link(nc.vector.tensor_copy(tot[:], misc[:, K * E:2 * K * E].rearrange("p (k e) -> p e k", k=K)))
                link(nc.vector.tensor_tensor_scan(run[:].rearrange("p e k -> p (e k)"), restart[:].rearrange("p e k -> p (e k)"),
                                                  tot[:].rearrange("p e k -> p (e k)"), 0.0, ALU.mult, ALU.add))
                link(nc.vector.tensor_scalar(cnt_i[:], run[:, :, K - 1], float(P - 1), None, ALU.add))
                link(nc.vector.tensor_scalar(til_i[:], cnt_i[:], 7, None, ALU.logical_shift_right))
                link(nc.vector.tensor_copy(til[:], til_i[:]))
                link(nc.vector.tensor_tensor_scan(end[:], ones[:, 0:E], til[:], 0.0, ALU.mult, ALU.add))
                link(nc.vector.tensor_tensor(beg[:], end[:], til[:], ALU.subtract))
                link(nc.vector.scalar_tensor_tensor(out=pos_a[:], in0=beg[:, :, None].to_broadcast([P, E, K]),
                                                    scalar=float(P), in1=run[:], op0=ALU.mult, op1=ALU.add))
                link(nc.vector.tensor_tensor(pos_b[:], pos_a[:], tot[:], ALU.subtract))
                nc.vector.tensor_tensor(pos_e[:], misc[:, 0:K * E].rearrange("p (k e) -> p k e", k=K),
                                        pos_b[:].rearrange("p e k -> p k e"), ALU.add).then_inc(s["prefix_used"], 1)

            def slots(b, i, _):
                link = chain(dve, s["slot_chain"], SLOT_LINKS, b)
                dve.wait_ge(s["prefix_used"], b + 1)
                nc.vector.tensor_copy(weight[:, i], best[:])
                for c in range(TOPK):
                    last = nc.vector.tensor_tensor(pos_h[:, c * K:(c + 1) * K], hot[:, c], pos_e[:], ALU.mult)
                link(last)
                link(nc.vector.tensor_reduce(pos_f[:], pos_h[:], AX.X, ALU.add))
                after(dve, gathered[i], turns(16 * TOPK * K, b, i))
                nc.vector.tensor_copy(pos[:, i], pos_f[:])
                link(nc.vector.tensor_tensor(past[:], iota_j[:], end[0:1, None, :].to_broadcast([1, TILES, E]), ALU.is_ge))
                link(nc.vector.tensor_reduce(exp_f[:], past[:], AX.X, ALU.add))
                after(dve, s["tile_out"], TILES * (b - 1))
                nc.vector.tensor_scalar(expert[:, i], exp_f[:], float(E - 1), None, ALU.min).then_inc(s["routed"], 1)

            def tile_turn(b, i, j):
                dve.wait_ge(s["tile_hi"], TILES * b + j + 1)
                nc.vector.tensor_tensor(xt_lo[:, (i + j) % 2], turn[:, 0:P], xt_hi[:, (i + j) % 2].bitcast(F32),
                                        ALU.subtract).then_inc(s["tile_lo"], 1)

            def mix_results(b, i, _):
                dve.wait_ge(gathered[i], turns(16 * TOPK * K, b, i) + 16 * TOPK * K)
                after(dve, s["written"], 16 * (b + 1))
                for k in range(K):
                    last = nc.vector.tensor_scalar(mix[:, k], yg[:, 0, k], weight[:, i, 0, k:k + 1], None, ALU.mult)
                last.then_inc(s["mix_half"], 1)
                dve.wait_ge(s["mix_half"], b + 1)
                for k in range(K):
                    last = nc.vector.scalar_tensor_tensor(out=mix[:, k], in0=yg[:, 1, k], scalar=weight[:, i, 1, k:k + 1],
                                                          in1=mix[:, k], op0=ALU.mult, op1=ALU.add)
                last.then_inc(s["mix_ready"], 1)

            def mix_stats(b, i, _):
                alone(dve, (s["mix_ready"], b + 1))
                moments(lambda k: mix[:, k, :], st_m, mv_m, K, s["mix_stats"], s["mix_mom"], b + 1)

            def result(b, i, _):
                dve.wait_ge(s["mix_scale"], b + 1)
                for k in range(K):
                    last = nc.vector.tensor_scalar(mix[:, k], mix[:, k], mv_m[:, k, 0:1], rs_m[:, k:k + 1],
                                                   ALU.subtract, ALU.mult)
                last.then_inc(s["results_free"], 1)

            nc.vector.memset(eps[:, 0:1], EPS)
            nc.vector.memset(eps[:, 1:2], EPS * EPS)
            nc.vector.memset(zeros[:], 0.0).then_inc(s["zero_set"], 1)
            nc.vector.memset(ones_b[:], 1.0).then_inc(s["results_free"], 1)
            nc.vector.memset(ones[:], 1.0).then_inc(s["dve_set"], 1)
            dve.wait_ge(x_loaded[0], 16)
            moments(lambda k: xs[:, 0, k, :], st, mv[:, 0], K, s["stats"], s["moments"], 1)
            norm(0, 0, 0)
            dve.wait_ge(s["small"], 16 * 10)
            nc.vector.tensor_copy(bias_parts[:, 0], bias_f[:]).then_inc(s["bias_split"], 1)
            dve.wait_ge(s["bias_split"], 1)
            nc.vector.tensor_tensor(bias_r[:], bias_f[:], bias_parts[:, 0], ALU.subtract).then_inc(s["bias_split"], 1)
            dve.wait_ge(s["bias_split"], 2)
            nc.vector.tensor_copy(bias_parts[:, 1], bias_r[:]).then_inc(s["bias_split"], 1)
            dve.wait_ge(s["bias_split"], 3)
            nc.vector.tensor_tensor(bias_s[:], bias_r[:], bias_parts[:, 1], ALU.subtract).then_inc(s["bias_split"], 1)
            dve.wait_ge(s["bias_split"], 4)
            nc.vector.tensor_copy(bias_parts[:, 2], bias_s[:]).then_inc(s["bias_split"], 1)
            nc.vector.tensor_copy(w_rep[:], w_bc[:].rearrange("d (c n) -> d c n", c=2)[:, :, :, None]
                                  .to_broadcast([D, 2, N, J])).then_inc(s["w_rep_set"], 1)
            dve.wait_ge(s["decay_exp"], 1)
            nc.vector.tensor_scalar(decay[:], decay[:], -1.0, None, ALU.mult).then_inc(s["decay_set"], 1)
            dve.wait_ge(s["pool_set"], 3)
            nc.vector.tensor_copy(spread[:], spread_f[:].rearrange("p a n j -> p a (n j)"))
            nc.vector.tensor_reduce(fold[:, FOLD_AT:FOLD_AT + J], fold_f[:].rearrange("p n j -> p j n"), AX.X, ALU.add)
            nc.vector.tensor_copy(iota_e[:], iota_i[:].rearrange("p (k e) -> p k e", k=K))
            nc.vector.tensor_copy(iota_j[:], iota_ji[:].rearrange("p (j e) -> p j e", e=E))
            nc.vector.tensor_scalar(restart[:], iota_k[:].rearrange("p (e k) -> p e k", e=E), 1.0, None,
                                    ALU.min).then_inc(s["consts"], 1)
            walk(dve, dict(stats=stats, norm=norm, skip=skip_path, dt=dt_gx, rest=rest, drive=drive, scan=scan,
                           weights=weights, y_sum=y_sum, y_norm=y_norm, x1_stats=x1_stats, x1_norm=x1_norm,
                           gate_max=gate_max, softmax=softmax, second=second, starts=starts, slots=slots, tile_turn=tile_turn,
                           mix=mix_results, mix_stats=mix_stats, result=result),
                 begun=("stats", "norm"))

        @block.tensor
        def _(pe):
            def turn_x(b, i, _):
                pe.wait_ge(s["normed"], b + 1)
                after(pe, s["c_ready"], b)
                after(pe, s["prefix_used"], b - 2)
                for k in range(K):
                    last = nc.tensor.matmul(misc[:, k * P:(k + 1) * P], xn[:, i, k], ident[:], start=True, stop=True,
                                            is_transpose=True)
                last.then_inc(s["turned"], 1)

            def states(b, i, _):
                pe.wait_ge(s["dt_ready"], b + 1)
                nc.tensor.matmul(misc[:], w_rep[:, 0].rearrange("d n j -> d (n j)"), xa[:, i], start=True,
                                 stop=True).then_inc(s["b_ps"], 1)

            def readout(b, i, _):
                pe.wait_ge(s["b_ready"], b + 1)
                nc.tensor.matmul(misc[:], w_rep[:, 1].rearrange("d n j -> d (n j)"), xa[:, i], start=True,
                                 stop=True).then_inc(s["c_ps"], 1)

            def delta(b, i, _):
                pe.wait_ge(s["xa_ready"], b + 1)
                nc.tensor.matmul(misc[:], w_dt[:], xa[:, i], start=True, stop=False)
                pe.wait_ge(s["bias_in"], 16)
                nc.tensor.matmul(misc[:], bias[:, BDT_AT:BDT_AT + D], ones_b[:], start=False, stop=True).then_inc(s["z_ps"], 1)

            def rep(b, i, r):
                n = UNITS * b + r
                if r == 0:
                    pe.wait_ge(stacked[i], turns(128, b, i) + 128)
                h, m = divmod(r, J)
                after(pe, s["decayed"], n)
                nc.tensor.matmul(dt_ps[:], spread[:, m], dt_s[:, i, h], start=True, stop=True).then_inc(s["dt_rep"], 1)
                after(pe, s["driven"], n)
                nc.tensor.matmul(gx_ps[:], spread[:, m], gx_s[:, i, h], start=True, stop=True).then_inc(s["gx_rep"], 1)

            def reduce(b, i, r):
                n = UNITS * b + r
                pe.wait_ge(s["weighed"], n + 1)
                if r == 0:
                    after(pe, s["y_copied"], b)
                nc.tensor.matmul(y_ps[:], fold[:, FOLD_AT - J * r:FOLD_AT - J * r + D], ch[:, r % NU], start=(r == 0),
                                 stop=(r == UNITS - 1)).then_inc(s["reduced"], 1)

            def y_turn(b, i, _):
                pe.wait_ge(s["y_copied"], b + 1)
                after(pe, s["tile_lo"], TILES * (b - 1))
                for k in range(K):
                    last = nc.tensor.matmul(turn[:, k * P:(k + 1) * P], yx_t[:, k * P:(k + 1) * P], ident[:], start=True,
                                            stop=True, is_transpose=True)
                last.then_inc(s["y_turned"], 1)

            def gate_turn(b, i, _):
                pe.wait_ge(s["x2_ready"], b + 1)
                pe.wait_ge(s["c_ready"], min(b + 3, SEQS) if isinstance(b, int) else b + 3)
                for k in range(K):
                    last = nc.tensor.matmul(misc[:, k * P:(k + 1) * P], x2[:, i, k], ident[:], start=True, stop=True,
                                            is_transpose=True)
                last.then_inc(s["x2_turned"], 1)

            def gate_logits(b, i, _):
                pe.wait_ge(s["x2_copied"], b + 1)
                for k in range(K):
                    last = nc.tensor.matmul(misc[:, k * E:(k + 1) * E], yx_t[:, k * P:(k + 1) * P], gate[:], start=True,
                                            stop=True)
                last.then_inc(s["logits_ps"], 1)

            def count(b, i, _):
                pe.wait_ge(s["mask_ready"], b + 1)
                m = mask[:].rearrange("p k e -> p (k e)")
                nc.tensor.matmul(misc[:, 0:K * E], before[:], m, start=True, stop=True)
                nc.tensor.matmul(misc[:, K * E:2 * K * E], ones[:], m, start=True, stop=True).then_inc(s["prefix_ready"], 1)

            def tile_turn(b, i, j):
                pe.wait_ge(tile_loaded[j % NX], 16 * (TILES // NX * b + j // NX + 1))
                after(pe, s["tile_lo"], TILES * b + j)
                if j == 0:
                    after(pe, s["y_ready"], min(b + 2, SEQS) if isinstance(b, int) else b + 2)
                nc.tensor.matmul(turn[:, 0:P], xt[:, j % NX], ident[:], start=True, stop=True,
                                 is_transpose=True).then_inc(s["tile_turned"], 1)

            picked = {}

            def begin():
                picked.clear()

            def pick(i, j):
                return pe.value_load(expert[0:1, i, j:j + 1], min_val=0, max_val=E - 1)

            def tile_pick(b, i, j):
                if j == 0:
                    alone(pe, (s["routed"], b + 1), (s["w_split_lo"], E), (s["w_ld"], 16))
                picked[i, j] = pick(i, j)

            def tile_up(b, i, j):
                e = picked[i, j] if (i, j) in picked else pick(i, j)
                picked[i, j] = e
                pe.wait_ge(s["tile_lo"], TILES * b + j + 1)
                after(pe, s["hid_ready"], TILES * b + j)
                nc.tensor.matmul(hid_ps[:], xt_lo[:, (i + j) % 2], w_hi[:, bass.ds(e * HID, HID)], start=True, stop=False)
                nc.tensor.matmul(hid_ps[:], xt_hi[:, (i + j) % 2], w_lo[:, bass.ds(e * HID, HID)], start=False, stop=False)
                nc.tensor.matmul(hid_ps[:], xt_hi[:, (i + j) % 2], w_hi[:, bass.ds(e * HID, HID)], start=False,
                                 stop=True).then_inc(s["tile_hid"], 1)

            def tile_fold(b, i, j):
                pe.wait_ge(s["hid_ready"], TILES * b + j + 1)
                after(pe, s["hid_t_ready"], TILES * b + j)
                for c in range(HC):
                    last = nc.tensor.matmul(fold_ps[:, c * P:(c + 1) * P], hid[:, (i + j) % 2, c * P:(c + 1) * P], ident[:],
                                            start=True, stop=True, is_transpose=True)
                last.then_inc(s["tile_folded"], 1)

            def tile_down(b, i, j):
                e = picked[i, j] if (i, j) in picked else pick(i, j)
                pe.wait_ge(s["hid_t_ready"], TILES * b + j + 1)
                after(pe, s["tile_copied"], TILES * b + j)
                o = out_ps[:, 0:D]
                nc.tensor.matmul(o, ones_b[:, 0:P], bias[:, bass.ds(e * D, D)], start=True, stop=False)
                for c in range(HC):
                    last = nc.tensor.matmul(o, hid_t[:, (i + j) % 2, c * P:(c + 1) * P], w2_f[:, bass.ds(e * HC * D + c * D, D)],
                                            start=False, stop=(c == HC - 1))
                last.then_inc(s["tile_out"], 1)

            pe.wait_ge(s["pool_set"], 2)
            turn_x(0, 0, 0)
            pe.wait_ge(s["pool_set"], 3)
            pe.wait_ge(s["w_rep_set"], 1)
            pe.wait_ge(s["consts"], 1)
            walk(pe, dict(begin=begin, tile_pick=tile_pick, turn=turn_x, states=states, readout=readout, delta=delta, rep=rep, reduce=reduce, y_turn=y_turn,
                          gate_turn=gate_turn, gate_logits=gate_logits, count=count, tile_turn=tile_turn,
                          tile_up=tile_up, tile_fold=tile_fold, tile_down=tile_down),
                 begun=("turn",))


def kernel(**inputs):
    import numpy as np
    import concourse.bacc as bacc
    from concourse.bass_utils import run_bass_kernel_spmd

    a = {k: np.asarray(v) for k, v in inputs.items()}
    arrays = {
        "x": a["L0_attn_x"],
        "w_dt_t": a["L0_attn_W_dt"].T,
        "w_bc_t": np.concatenate([a["L0_attn_W_B"], a["L0_attn_W_C"]]).T,
        "biases": np.concatenate([a["L0_ffn_b2"].ravel(), a["L0_attn_b_dt"]]),
        "b1": a["L0_ffn_b1"].reshape(E * HC, P).T,
        "d_param": a["L0_attn_D_param"],
        "a_log": a["L0_attn_A_log"].reshape(UNITS, J, N).transpose(2, 1, 0).reshape(P, UNITS),
        "gamma": a["L0_attn_gamma"],
        "beta": a["L0_attn_beta"],
        "gate_w": a["L0_ffn_gate_w"],
        "gate_b": a["L0_ffn_gate_b"],
        "w1": a["L0_ffn_w1"],
        "w2": a["L0_ffn_w2"],
    }
    arrays = {k: np.ascontiguousarray(v) for k, v in arrays.items()}
    nc = bacc.Bacc("TRN2", target_bir_lowering=False, num_devices=1)
    args = [nc.dram_tensor(k, v.shape, mybir.dt.from_np(v.dtype), kind="ExternalInput").ap() for k, v in arrays.items()]
    out = nc.dram_tensor("out", (SEQS, T, D), F32, kind="ExternalOutput").ap()
    program(nc, *args, out)
    result = run_bass_kernel_spmd(nc, [arrays], core_ids=[0])
    return result.results[0]["out"]
```
